# Optimizing a Trainium2 kernel written in Bass

```python
import numpy as np
import jax
import jax.numpy as jnp

def _softmax(x, axis=-1):
    return jax.nn.softmax(x, axis=axis)

def _gelu(x):
    return jax.nn.gelu(x, approximate=True)

def _silu(x):
    return jax.nn.silu(x)

def _sigmoid(x):
    return jax.nn.sigmoid(x)

def _layernorm(x, axis=-1, eps=1e-05):
    m = jnp.mean(x, axis=axis, keepdims=True)
    v = jnp.var(x, axis=axis, keepdims=True)
    return (x - m) / jnp.sqrt(v + eps)

def _scatter_add(tgt, idx, src, axis=0):
    return tgt.at[idx].add(src)

def _segment_sum(src, seg, n):
    return jax.ops.segment_sum(src, seg, n)
kernel_name = 'mk_adj_preln_d4_adj_r2_de0d44'

def setup_inputs(seed: int=0):
    np.random.seed(seed)
    _w = jnp.asarray

    def _rec_inputs():
        import jax
        import jax.numpy as jnp
        _gk = jax.random.key(seed)
        x = -0.0002928 + 1 * jax.random.normal(jax.random.fold_in(_gk, 1), (2048, 256), jnp.float32)
        _w = (1.0 + jnp.arange(2048, dtype=jnp.float32)) ** (-0.5)
        _w = _w / _w.mean()
        _pij = jnp.clip(0.000976562 * _w[:, None] * _w[None, :], 0.0, 1.0)
        _a = jax.random.uniform(jax.random.fold_in(_gk, 2), (2048, 2048)) < _pij
        _a = jnp.logical_or(_a, jnp.eye(2048, dtype=bool))
        _af = _a.astype(jnp.float32)
        _af = _af * jax.random.uniform(jax.random.fold_in(_gk, 3), (2048, 2048), jnp.float32, 0.05, 1)
        adj = _af
        return (x, adj)
    x, adj = _rec_inputs()

    def _L0_gnn_setup():
        import jax, jax.numpy as jnp
        import numpy as np
        IN_F = 256
        OUT_F = 256
        N = 4096
        key = jax.random.key(seed)
        k1, k2, k3 = jax.random.split(key, 3)
        x = jax.random.normal(k1, (N, IN_F), dtype=jnp.float32)
        graph = jax.random.uniform(k2, (N, N), dtype=jnp.float32)
        std = float(np.sqrt(2.0 / (IN_F + OUT_F)))
        weight = jax.random.normal(k3, (IN_F, OUT_F), dtype=jnp.float32) * std
        bias = jnp.zeros((OUT_F,), dtype=jnp.float32)
        return {'x': x, 'graph': graph, 'weight': weight, 'bias': bias}
    _L0_gnn_all = _L0_gnn_setup()
    _L0_gnn_in = {k: v for k, v in _L0_gnn_all.items() if k in ('weight', 'bias')}
    del _L0_gnn_all

    def _L1_gnn_setup():
        import jax, jax.numpy as jnp
        import numpy as np
        N = 4096
        D = 256
        EPS = 1e-12
        key = jax.random.key(seed)
        k1, k2 = jax.random.split(key)
        cur = jax.random.normal(k1, (N, D), dtype=jnp.float32)
        incidence_m = jax.random.normal(k2, (N, N), dtype=jnp.float32)
        return {'cur': cur, 'incidence_m': incidence_m}
    _L1_gnn_all = _L1_gnn_setup()
    _L1_gnn_in = {k: v for k, v in _L1_gnn_all.items() if k in ()}
    del _L1_gnn_all

    def _L2_gnn_setup():
        import jax, jax.numpy as jnp
        import numpy as np
        N_HEADS = 4
        N_HIDDEN = 256
        SLOPE = 0.01
        NEG = -1000000000.0
        key = jax.random.key(seed)
        k1, k2, k3, k4 = jax.random.split(key, 4)
        N, F_IN = (4096, 256)
        h = jax.random.normal(k1, (N, F_IN), dtype=jnp.float32)
        W = jax.random.normal(k2, (F_IN, N_HIDDEN * N_HEADS), dtype=jnp.float32) * 0.05
        a = jax.random.normal(k3, (N_HEADS, 2 * N_HIDDEN, 1), dtype=jnp.float32) * 0.05
        adj_mat = jnp.where(jax.random.uniform(k4, (N, N)) < 0.01, 0.0, NEG).astype(jnp.float32)
        return {'h': h, 'adj_mat': adj_mat, 'W': W, 'a': a}
    _L2_gnn_all = _L2_gnn_setup()
    _L2_gnn_in = {k: v for k, v in _L2_gnn_all.items() if k in ('W', 'a')}
    del _L2_gnn_all

    def _L3_gnn_setup():
        import jax, jax.numpy as jnp
        import numpy as np

        def _bin_sign(v):
            return jnp.sign(v)

        def _bin_sign_z(v):
            return jnp.maximum(jnp.sign(v), 0.0)
        key = jax.random.key(seed)
        k1, k2, k3 = jax.random.split(key, 3)
        N, D_IN, D_OUT = (4096, 256, 256)
        x = jax.random.normal(k1, (N, D_IN), dtype=jnp.float32)
        support = jax.random.uniform(k2, (N, N), dtype=jnp.float32)
        weight = jax.random.normal(k3, (D_OUT, D_IN), dtype=jnp.float32)
        return {'x': x, 'support': support, 'weight': weight}
    _L3_gnn_all = _L3_gnn_setup()
    _L3_gnn_in = {k: v for k, v in _L3_gnn_all.items() if k in ('weight',)}
    del _L3_gnn_all
    return {'x': x, 'adj': adj, 'L0_gnn_weight': _L0_gnn_in['weight'], 'L0_gnn_bias': _L0_gnn_in['bias'], 'L2_gnn_W': _L2_gnn_in['W'], 'L2_gnn_a': _L2_gnn_in['a'], 'L3_gnn_weight': _L3_gnn_in['weight']}

def reference(x, adj, L0_gnn_weight, L0_gnn_bias, L2_gnn_W, L2_gnn_a, L3_gnn_weight):
    import jax
    import jax.numpy as jnp

    def _L0_gnn_ref(x, graph, weight, bias):
        import jax, jax.numpy as jnp
        import numpy as np
        IN_F = 256
        OUT_F = 256
        N = 4096
        gt = graph.T
        deg = jnp.sum(gt, axis=1)
        d_inv_sqrt = deg ** (-0.5)
        norm = d_inv_sqrt[:, None] * gt * d_inv_sqrt[None, :]
        h = x @ weight
        y = norm @ h + bias
        return y

    def _L1_gnn_ref(cur, incidence_m):
        import jax, jax.numpy as jnp
        import numpy as np
        N = 4096
        D = 256
        EPS = 1e-12
        mask = incidence_m > 0
        head = jax.lax.stop_gradient(mask.astype(incidence_m.dtype))
        head = head / jnp.maximum(jnp.sqrt(jnp.sum(head * head, axis=-1, keepdims=True)), EPS)
        inc = incidence_m + head
        edge_fea = inc @ cur
        edge_degree = jnp.sum(inc, axis=-1, keepdims=True)
        return edge_fea / edge_degree

    def _L2_gnn_ref(h, adj_mat, W, a):
        import jax, jax.numpy as jnp
        import numpy as np
        N_HEADS = 4
        N_HIDDEN = 256
        SLOPE = 0.01
        NEG = -1000000000.0
        N = h.shape[0]
        ht = (h @ W).reshape(N, N_HEADS, N_HIDDEN).transpose(1, 0, 2)
        a_src = a[:, :N_HIDDEN, 0]
        a_dst = a[:, N_HIDDEN:, 0]
        src = jnp.einsum('hnd,hd->hn', ht, a_src)
        dst = jnp.einsum('hnd,hd->hn', ht, a_dst)
        e = jax.nn.leaky_relu(src[:, :, None] + dst[:, None, :], SLOPE) + adj_mat[None]
        att = jax.nn.softmax(e, axis=-1)
        h_prime = jnp.einsum('hij,hjd->hid', att, ht)
        return h_prime.mean(axis=0)

    def _L3_gnn_ref(x, support, weight):
        import jax, jax.numpy as jnp
        import numpy as np

        def _bin_sign(v):
            return jnp.sign(v)

        def _bin_sign_z(v):
            return jnp.maximum(jnp.sign(v), 0.0)
        bw = _bin_sign(weight)
        ba = _bin_sign_z(x)
        xw = ba @ bw.T
        out = support @ xw
        return jax.nn.relu(out)
    h = jnp.maximum(_layernorm(x, axis=-1), 0.0)
    x = x + _L0_gnn_ref(h, adj, L0_gnn_weight, L0_gnn_bias)
    h = jnp.maximum(_layernorm(x, axis=-1), 0.0)
    x = x + _L1_gnn_ref(h, adj)
    h = jnp.maximum(_layernorm(x, axis=-1), 0.0)
    x = x + _L2_gnn_ref(h, adj, L2_gnn_W, L2_gnn_a)
    h = jnp.maximum(_layernorm(x, axis=-1), 0.0)
    x = x + _L3_gnn_ref(h, adj, L3_gnn_weight)
    return x

_drawn_inputs = setup_inputs


def setup_inputs(seed=0):
    import zlib

    import numpy as np

    out = dict(_drawn_inputs(seed))
    spreads = {'L0_gnn_bias': (0.0, 0.1)}
    factors = {}
    for name, (base, spread) in spreads.items():
        noise = np.random.default_rng([zlib.crc32(name.encode()), seed]).standard_normal(out[name].shape)
        drawn = base * np.exp(spread * noise) if base else spread * noise
        out[name] = jnp.asarray(drawn.astype(out[name].dtype))
    for name, factor in factors.items():
        out[name] = (out[name] * factor).astype(out[name].dtype)
    return out
```

```python
from contextlib import ExitStack

import concourse.bass as bass
from concourse import mybir

F32 = mybir.dt.float32
F16 = mybir.dt.float16
ALU = mybir.AluOpType
ACT = mybir.ActivationFunctionType
AX_X = mybir.AxisListType.X
RMAX = bass.bass_isa.ReduceOp.max

P = 128
KB = 1024
ADJ_SCALE = 256.0
H_SCALE = 16.0
W_SCALE = 16.0
P_SCALE = 4096.0
LN_EPS = 1e-5
NORM_EPS = 1e-12
SLOPE = 0.01


def gnn_stack(nc, x_d, adj_d, w0_d, b0_d, w2_d, a2_d, w3_d, out_d):
    N, D = x_d.shape
    NB = N // P
    DC = D // P
    HEADS = a2_d.shape[0]
    HD = HEADS * D
    DE = D + 1
    DS = D + 2
    QB = 4
    NQ = NB // QB
    HALF = N // 2
    HBK = NB // 2
    TG = 4

    x_rows = x_d.rearrange("(t p) d -> p t d", p=P)
    out_rows = out_d.rearrange("(t p) d -> t p d", p=P)
    adj_rows = adj_d.rearrange("(t p) n -> t p n", p=P)

    at_dram = nc.dram_tensor("adj_t_parts", (NB, P, 2 * N), F16, kind="Internal").ap()
    e_dram = nc.dram_tensor("exp_adj_t", (NB, NB, P, P), F32, kind="Internal").ap()
    u_dram = nc.dram_tensor("u_rows", (NB, HEADS, P), F32, kind="Internal").ap()

    with ExitStack() as ctx:
        def sb(name, shape, dt):
            return ctx.enter_context(nc.sbuf_tensor(name, shape, dt))

        def sem(name):
            return ctx.enter_context(nc.semaphore(name))

        x = sb("x", [P, NB, D], F32)
        ident = sb("ident", [P, P], F32)
        ident16 = sb("ident16", [P, P], F16)
        ones16 = sb("ones16", [P, P], F16)
        row_pair = sb("row_pair", [P, 2, D], F32)
        bias = row_pair[:, 0, :]
        head_out = row_pair
        bw_t = sb("bw_t", [P, DC, D], F16)
        neg_half = sb("neg_half", [P, NB], F32)
        stats = sb("stats", [P, NB, 6], F32)
        mean_var = sb("mean_var", [P, NB, 2], F32)
        var_eps = sb("var_eps", [P, NB], F32)
        rstd = sb("rstd", [P, NB], F32)
        deg = sb("deg", [P, NB], F32)
        dinv = sb("dinv", [P, NB], F32)
        dinv_in = sb("dinv_in", [P, NB], F32)
        dinv_out = sb("dinv_out", [P, NB], F32)
        wa_hi = sb("wa_hi", [P, DC, 2 * HEADS], F16)
        wa_lo = sb("wa_lo", [P, DC, 2 * HEADS], F16)
        wa = sb("wa", [P, DC, 2 * HEADS], F32)
        amax = sb("amax", [P, 4], F32)
        row_n = sb("row_n", [P, 2, 10], F32)
        held_act = sb("held_act", [P, 2 * QB], F32)
        held = sb("held", [P, 4], F32)
        sd = sb("sd", [P, NB, 2 * HEADS], F32)
        dmax = sb("dmax", [P, 3, HEADS], F32)
        w_j = sb("w_j", [P, NB, HEADS], F32)
        vp_j = sb("vp_j", [P, NB, HEADS], F32)
        up_i = sb("up_i", [P, NB, HEADS], F32)
        neg_mean = sb("neg_mean", [P, QB], F32)
        inv_l = sb("inv_l", [P, 2, QB], F32)

        ARENA = 184 * KB + 512
        arena = sb("arena", [P, ARENA // 4], F32)

        def view(off, shape, dt):
            size = 4 if dt == F32 else 2
            n = 1
            for s in shape:
                n *= s
            words = (n * size + 3) // 4
            v = arena[:, off // 4:off // 4 + words]
            if dt == F16:
                v = v.bitcast(F16)
            if len(shape) == 1:
                return v
            names = " ".join("abcd"[:len(shape)])
            return v.rearrange(f"p ({names}) -> p {names}", **{"abcd"[k]: s for k, s in enumerate(shape)})

        nat = view(0, [NB, 2, NB, P], F16)
        G0 = 128 * KB
        g_hi = view(G0, [NB, D], F16)
        g_lo = view(G0 + 8 * KB, [NB, D], F16)
        w0_f = view(G0, [DC, D], F32)
        w0_hi = view(G0 + 2 * KB, [DC, D], F16)
        w0_lo = view(G0 + 3 * KB, [DC, D], F16)
        w3_f = view(G0 + 4 * KB, [DC, D], F32)
        w3_s = view(G0 + 6 * KB, [DC, D], F16)
        hrelu = view(G0 + 8 * KB, [2, D], F32)
        hn_hi = view(G0 + 10 * KB, [2, D], F16)
        hn_lo = view(G0 + 11 * KB, [2, D], F16)
        h0_t = view(G0 + 12 * KB, [2, 2 * DC, P], F16)
        H1 = 144 * KB
        hw = view(H1, [NB, D], F32)
        h1_hi = view(H1, [NB, DS], F16)
        h1_lo = view(H1 + NB * DS * 2, [NB, D], F16)
        STG = 162 * KB
        stage = view(STG, [4, HALF], F32)
        LN = 178 * KB
        ln_relu = view(LN, [2, D], F32)
        nat_max = view(LN + 2 * KB, [N], F16)
        JUNK = 12
        junk = view(LN, [JUNK, P], F32)
        HT = HEADS * NB * DS * 2
        H2T = 2 * HT + 48 * KB
        at = view(0, [2, 2, NB, P], F16)
        mask = view(16 * KB, [2, NB, P], F16)
        e_out = view(24 * KB, [2, NB, P], F32)
        w2_f = view(56 * KB, [DC, HD], F32)
        a_bc = view(64 * KB, [HEADS * 2 * D], F32)
        wa_junk = view(72 * KB, [D], F32)
        h2_hi = view(74 * KB, [2, D], F16)
        h2_lo = view(75 * KB, [2, D], F16)
        h2_t = view(H2T, [2 * DC, N], F16)
        w2_hi = view(H2T + 16 * KB, [DC, HD], F16)
        w2_lo = view(H2T + 20 * KB, [DC, HD], F16)
        ht_hi = view(0, [HEADS, NB, DS], F16)
        ht_lo = view(HT, [HEADS, NB, DS], F16)
        PR = 2 * HT
        prob = view(PR, [4, QB * P], F32)
        p_hi = view(PR + 8 * KB, [4, QB * P], F16)
        p_lo = view(PR + 12 * KB, [4, QB * P], F16)
        U = PR + 16 * KB
        u_bc = view(U, [HEADS, N], F32)
        RING3 = U + 32 * KB
        at3 = view(RING3, [4, 2, NB, P], F16)
        ba = view(RING3 + 32 * KB, [NB, D], F16)
        up_t = view(RING3 + 32 * KB, [P], F32)
        e_in = view(RING3 + 40 * KB, [NB, QB * P], F32)
        ba_t = view(0, [2, DC, P], F16)
        xw = view(2 * KB, [NB, D], F16)

        ps = ctx.enter_context(nc.psum_tensor("ps", [P, 8, 512], F32))

        def ps16(bank):
            return ps[:, bank, :].bitcast(F16)

        x_in = sem("x_in")
        w0_in = sem("w0_in")
        w2_in = sem("w2_in")
        consts = sem("consts")
        ident_zero = sem("ident_zero")
        half_in = [sem(f"half_in{k}") for k in range(4)]
        nat_hi_done = sem("nat_hi_done")
        nat_lo_done = sem("nat_lo_done")
        deg_done = sem("deg_done")
        max_made = sem("max_made")
        ht_ones = sem("ht_ones")
        sum4 = sem("sum4")
        dv = sem("dv")
        stats_done = sem("stats_done")
        rstd_done = sem("rstd_done")
        w3_signed = sem("w3_signed")
        w3_t_ps = sem("w3_t_ps")
        w3_t_done = sem("w3_t_done")
        w0_hi_done = sem("w0_hi_done")
        w0_lo_done = sem("w0_lo_done")
        relu0 = sem("relu0")
        h0_hi_done = sem("h0_hi_done")
        h0_lo_done = sem("h0_lo_done")
        h0_t_ps = sem("h0_t_ps")
        h0_t_done = sem("h0_t_done")
        hw_ps = sem("hw_ps")
        hw_done = sem("hw_done")
        deg_copied = sem("deg_copied")
        dinv_done = sem("dinv_done")
        dinv_scaled = sem("dinv_scaled")
        g_hi_done = sem("g_hi_done")
        g_lo_done = sem("g_lo_done")
        y_ps = sem("y_ps")
        y_taken = sem("y_taken")
        dl = sem("dl")
        ve1 = sem("ve1")
        rs1 = sem("rs1")
        relu1 = sem("relu1")
        h1_hi_done = sem("h1_hi_done")
        h1_lo_done = sem("h1_lo_done")
        ones_col = sem("ones_col")
        amax_part = sem("amax_part")
        amax_all = sem("amax_all")
        amax_neg = sem("amax_neg")
        t_ps = sem("t_ps")
        at_hi_done = sem("at_hi_done")
        e_done = sem("e_done")
        at_lo_done = sem("at_lo_done")
        mask_done = sem("mask_done")
        at_sent = [sem(f"at_sent{b}") for b in range(2)]
        e_sent = [sem(f"e_sent{b}") for b in range(2)]
        l1_ps = sem("l1_ps")
        l1_taken = sem("l1_taken")
        dm = sem("dm")
        n_done = sem("n_done")
        c_done = sem("c_done")
        ve2 = sem("ve2")
        rs2 = sem("rs2")
        relu2 = sem("relu2")
        h2_hi_done = sem("h2_hi_done")
        h2_lo_done = sem("h2_lo_done")
        h2_t_ps = sem("h2_t_ps")
        h2_t_done = sem("h2_t_done")
        wa_done = sem("wa_done")
        w2_hi_done = sem("w2_hi_done")
        w2_lo_done = sem("w2_lo_done")
        sd_ps = sem("sd_ps")
        dmax_part = sem("dmax_part")
        dmax_all = sem("dmax_all")
        d_shift = sem("d_shift")
        up_arg = sem("up_arg")
        exps = sem("exps")
        scaled_w = sem("scaled_w")
        scaled_u = sem("scaled_u")
        ut_ps = sem("ut_ps")
        ut_done = sem("ut_done")
        u_out = sem("u_out")
        u_in = [sem(f"u_in{h}") for h in range(HEADS)]
        ht_ps = sem("ht_ps")
        ht_hi_done = sem("ht_hi_done")
        ht_lo_done = sem("ht_lo_done")
        e_loaded = [sem(f"e_loaded{k}") for k in range(NB // TG)]
        p_done = sem("p_done")
        p_hi_done = sem("p_hi_done")
        p_lo_done = sem("p_lo_done")
        p_used = sem("p_used")
        att_ps = sem("att_ps")
        inv_done = sem("inv_done")
        head_scaled = sem("head_scaled")
        head_added = sem("head_added")
        ba_chain = sem("ba_chain")
        ba_done = sem("ba_done")
        at3_in = [sem(f"at3_in{k}") for k in range(4)]
        ba_t_ps = sem("ba_t_ps")
        ba_t_done = sem("ba_t_done")
        xw_ps = sem("xw_ps")
        xw_done = sem("xw_done")
        o_ps = sem("o_ps")
        o_done = sem("o_done")
        out_sent = sem("out_sent")

        block = ctx.enter_context(nc.Block())

        @block.sync
        def _(sp):
            sp.dma_start(x[:, :, :], x_rows).then_inc(x_in, 16)
            sp.dma_start(w0_f, w0_d.rearrange("(c p) d -> p c d", p=P)).then_inc(w0_in, 16)
            sp.dma_start(w3_f, w3_d.rearrange("(c p) d -> p c d", p=P)).then_inc(w0_in, 16)
            sp.dma_start(bias, b0_d.partition_broadcast(P)).then_inc(w0_in, 16)

            def load_pass1(i, first):
                for b in range(2):
                    for s in range(2):
                        k = 2 * b + s
                        if not first:
                            sp.wait_ge(nat_lo_done, 4 * i + k - 3)
                        sp.dma_start(stage[:, k, :], adj_rows[2 * i + b][:, s * HALF:(s + 1) * HALF]
                                     ).then_inc(half_in[k], 16)

            load_pass1(0, True)
            with nc.sync.Fori(1, NB // 2) as i:
                load_pass1(i, False)

            def load_pass2(i, b, first):
                if True:
                    for s in range(2):
                        k = 2 * b + s
                        if first:
                            sp.wait_ge(nat_lo_done, 4 * (NB // 2 - 1) + k + 1)
                        else:
                            sp.wait_ge(t_ps, 2 * (4 * (i - 1) + k) + 2)
                        sp.dma_start(stage[:, k, :], adj_rows[2 * i + b][:, s * HALF:(s + 1) * HALF]
                                     ).then_inc(half_in[k], 16)

            def store_block(i, b):
                sp.wait_ge(at_lo_done, 4 * (2 * i + b) + 4)
                sp.dma_start(at_dram[2 * i + b], at[:, b, :, :, :].rearrange("p h j n -> p (h j n)")
                             ).then_inc(at_sent[b], 16)
                sp.wait_ge(e_done, 4 * (2 * i + b) + 4)
                sp.dma_start(e_dram[2 * i + b].rearrange("j p n -> p j n"), e_out[:, b, :, :]
                             ).then_inc(e_sent[b], 16)

            for b in range(2):
                load_pass2(0, b, True)
            sp.wait_ge(y_ps, 10)
            sp.wait_ge(amax_part, 1)
            sp.dma_start(w2_f, w2_d.rearrange("(c p) m -> p c m", p=P)).then_inc(w2_in, 16)
            sp.dma_start(a_bc, a2_d.rearrange("h e o -> (h e o)").partition_broadcast(P)
                         ).then_inc(w2_in, 16)
            with nc.sync.Fori(1, NB // 2) as i:
                for b in range(2):
                    load_pass2(i, b, False)
                    store_block(i - 1, b)
            for b in range(2):
                store_block(NB // 2 - 1, b)

            sp.wait_ge(ut_done, 1)
            sp.dma_start(u_dram.rearrange("t h n -> (t h) n"), up_t[0:HEADS * NB, :]).then_inc(u_out, 16)
            sp.wait_ge(u_out, 16)
            for h in range(HEADS):
                sp.dma_start(u_bc[:, h, :].rearrange("p (t n) -> p t n", t=NB),
                             u_dram[:, h, :].partition_broadcast(P)).then_inc(u_in[h], 16)

            e_q = e_dram.rearrange("(q r) (g j) p n -> q g j p r n", r=QB, j=TG)

            def load_e(q, first):
                for g in range(NB // TG):
                    if not first:
                        sp.wait_ge(p_done, (q - 1) * HEADS * NB + (HEADS - 1) * NB + TG * (g + 1))
                    for j in range(TG):
                        sp.dma_start(e_in[:, TG * g + j, :].rearrange("p (r n) -> p r n", r=QB),
                                     e_q[q, g, j]).then_inc(e_loaded[g], 16)

            for b in range(2):
                sp.wait_ge(e_sent[b], 16 * NB // 2)
                sp.wait_ge(at_sent[b], 16 * NB // 2)
            sp.wait_ge(l1_ps, NB)
            sp.wait_ge(h2_lo_done, NB)
            load_e(0, True)
            with nc.sync.Fori(1, NQ) as q:
                load_e(q, False)

            sp.wait_ge(ht_ps, 2 * NB)
            for k in range(4):
                sp.dma_start(at3[:, k, :, :, :].rearrange("p h j n -> p (h j n)"), at_dram[k]
                             ).then_inc(at3_in[k], 16)

            def store_out(i, k):
                sp.wait_ge(o_done, 4 * i + k + 1)
                sp.dma_start(out_rows[4 * i + k], x[:, 4 * i + k, :]).then_inc(out_sent, 16)

            with nc.sync.Fori(1, NB // 4) as i:
                for k in range(4):
                    sp.wait_ge(o_ps, 4 * i + k - 3)
                    sp.dma_start(at3[:, k, :, :, :].rearrange("p h j n -> p (h j n)"), at_dram[4 * i + k]
                                 ).then_inc(at3_in[k], 16)
                    store_out(i - 1, k)
            for k in range(4):
                store_out(NB // 4 - 1, k)
            sp.wait_ge(out_sent, 16 * NB)

        @block.gpsimd
        def _(pool):
            nc.gpsimd.memset(ident[:, :], 0.0).then_inc(ident_zero, 1)
            nc.gpsimd.memset(ones16[:, :], 1.0).then_inc(consts, 1)
            nc.gpsimd.memset(neg_half[:, :], -0.5).then_inc(consts, 1)
            pool.wait_ge(ident_zero, 1)
            nc.gpsimd.affine_select(out=ident[:, :], in_=ident[:, :], compare_op=ALU.not_equal, fill=1.0,
                                    base=0, pattern=[[-1, P]], channel_multiplier=1).then_inc(ident_zero, 1)
            pool.wait_ge(ident_zero, 2)
            nc.gpsimd.tensor_copy(ident16[:, :], ident[:, :]).then_inc(consts, 1)
            pool.wait_ge(consts, 3)

            pool.wait_ge(stats_done, 1)
            nc.gpsimd.tensor_tensor(rstd[:, :], var_eps[:, :], neg_half[:, :], ALU.pow).then_inc(rstd_done, 1)
            pool.wait_ge(deg_copied, 1)
            nc.gpsimd.tensor_tensor(dinv[:, :], deg[:, :], neg_half[:, :], ALU.pow).then_inc(dinv_done, 1)

            for half in range(2):
                with nc.gpsimd.Fori(half * HBK, (half + 1) * HBK) as i:
                    pool.wait_ge(ve1, i + 1)
                    nc.gpsimd.tensor_tensor(rstd[:, bass.ds(i, 1)], var_eps[:, bass.ds(i, 1)],
                                            neg_half[:, 0:1], ALU.pow).then_inc(rs1, 1)
                if half == 0:
                    pool.wait_ge(amax_part, 1)
                    nc.gpsimd.partition_all_reduce(amax[:, 1:2], amax[:, 0:1], P, RMAX).then_inc(amax_all, 1)
            with nc.gpsimd.Fori(0, NB // 2) as i:
                for b in range(2):
                    pool.wait_ge(n_done, 2 * i + b + 1)
                    nc.gpsimd.tensor_tensor(row_n[:, b, 1:2], row_n[:, b, 0:1], neg_half[:, 0:1],
                                            ALU.pow).then_inc(c_done, 1)
                    pool.wait_ge(ve2, 2 * i + b + 1)
                    nc.gpsimd.tensor_tensor(row_n[:, b, 7:8], row_n[:, b, 6:7], neg_half[:, 0:1],
                                            ALU.pow).then_inc(rs2, 1)

            pool.wait_ge(dmax_part, 1)
            nc.gpsimd.partition_all_reduce(dmax[:, 1, :], dmax[:, 0, :], P, RMAX).then_inc(dmax_all, 1)

            with nc.gpsimd.Fori(0, NQ) as q:
                with nc.gpsimd.Fori(0, HEADS) as h:
                    for r in range(QB):
                        pool.wait_ge(head_scaled, q * (HEADS * QB) + h * QB + r + 1)
                        nc.gpsimd.tensor_tensor(x[:, QB * q + r, :], x[:, QB * q + r, :],
                                                head_out[:, r % 2, :], ALU.add).then_inc(head_added, 1)

        @block.tensor
        def _(pe):
            mm = nc.tensor.matmul
            pe.wait_ge(consts, 3)

            pe.wait_ge(w3_signed, 1)
            for c in range(DC):
                for oc in range(DC):
                    ins = nc.tensor.transpose(ps16(0)[:, (c * DC + oc) * P:(c * DC + oc + 1) * P],
                                              w3_s[:, oc, c * P:(c + 1) * P], ident16[:, :])
            ins.then_inc(w3_t_ps, 1)

            def degrees(j, first, last):
                pe.wait_ge(nat_lo_done, 2 * j + 2)
                for q in range(4):
                    for part in range(2):
                        ins = mm(ps[:, 4 + q, :].rearrange("p (a n) -> p a n", a=4), ones16[:, :],
                                 nat[:, 4 * q:4 * q + 4, part, j, :],
                                 start=(first and part == 0), stop=(last and part == 1))
                return ins

            def h0_transposes(t, b):
                pe.wait_ge(h0_lo_done, t + 1)
                pe.wait_ge(h0_hi_done, t + 1)
                for part, src in enumerate((hn_hi, hn_lo)):
                    for c in range(DC):
                        ins = nc.tensor.transpose(ps16(b)[:, (part * DC + c) * P:(part * DC + c + 1) * P],
                                                  src[:, b, c * P:(c + 1) * P], ident16[:, :])
                ins.then_inc(h0_t_ps, 1)

            def h0_products(t, b, first):
                pe.wait_ge(h0_t_done, t + 1)
                if not first:
                    pe.wait_ge(hw_done, t - 1)
                n = 0
                for ha, wb in ((0, w0_hi), (0, w0_lo), (1, w0_hi)):
                    for c in range(DC):
                        ins = mm(ps[:, 2 + b, 0:D], h0_t[:, b, ha * DC + c, :], wb[:, c, :],
                                 start=(n == 0), stop=(n == 5))
                        n += 1
                ins.then_inc(hw_ps, 1)

            pe.wait_ge(w3_t_done, 1)
            pe.wait_ge(w0_lo_done, 1)

            def load_step(i, first, last):
                for b in range(2):
                    t = 2 * i + b
                    if not (last and b == 1):
                        h0_transposes(t + 1, 1 - b)
                    h0_products(t, b, first)
                    if not (first and b == 0):
                        degrees(t - 1, first and b == 1, False)

            h0_transposes(0, 0)
            load_step(0, True, False)
            with nc.tensor.Fori(1, NB // 2 - 1) as i:
                load_step(i, False, False)
            load_step(NB // 2 - 1, False, True)
            degrees(NB - 1, False, True).then_inc(deg_done, 1)

            def layer0(i, first, only=(0, 1)):
                for b in only:
                    ib = 2 * i + b
                    if not first:
                        pe.wait_ge(y_taken, 2 * i + b - 1)
                    for j in range(NB):
                        if first and b == 0:
                            pe.wait_ge(g_lo_done, j + 1)
                        mm(ps[:, b, 0:D], nat[:, ib, 0, j, :], g_hi[:, j, :], start=(j == 0), stop=False)
                        mm(ps[:, b, 0:D], nat[:, ib, 0, j, :], g_lo[:, j, :], start=False, stop=False)
                        ins = mm(ps[:, b, 0:D], nat[:, ib, 1, j, :], g_hi[:, j, :], start=False,
                                 stop=(j == NB - 1))
                    ins.then_inc(y_ps, 1)

            layer0(0, True)
            with nc.tensor.Fori(1, NB // 2 - 1) as i:
                layer0(i, False)

            def transpose_group(i, b, g, first):
                if g % 2 == 0:
                    k = 2 * b + g // 2
                    pe.wait_ge(half_in[k], 16 * (NB // 2) + 16 * (i + 1))
                if not (first and g < 2):
                    n = 4 * (2 * i + b) + g
                    pe.wait_ge(mask_done, n - 1)
                    pe.wait_ge(e_done, n - 1)
                for a in range(TG):
                    jb = TG * g + a
                    ins = nc.tensor.transpose(ps[:, 4 + g % 2, a * P:(a + 1) * P],
                                              stage[:, 2 * b + g // 2, (jb % HBK) * P:(jb % HBK + 1) * P],
                                              ident[:, :])
                ins.then_inc(t_ps, 1)

            def products1(i, b, g, first):
                ib = 2 * i + b
                pe.wait_ge(mask_done, 4 * ib + g + 1)
                if g == 0 and not first:
                    pe.wait_ge(l1_taken, ib - 1)
                for a in range(TG):
                    j = TG * g + a
                    if first and b == 0:
                        pe.wait_ge(h1_lo_done, j + 1)
                        if j == 0:
                            pe.wait_ge(ones_col, 1)
                            pe.wait_ge(y_taken, NB)
                    s, e = (j == 0), (j == NB - 1)
                    mm(ps[:, 2 * b, 0:DE], at[:, b, 0, j, :], h1_hi[:, j, 0:DE], start=s, stop=False)
                    mm(ps[:, 2 * b, 0:D], at[:, b, 0, j, :], h1_lo[:, j, :], start=False, stop=False)
                    mm(ps[:, 2 * b, 0:DE], at[:, b, 1, j, :], h1_hi[:, j, 0:DE], start=False, stop=e)
                    mm(ps[:, 2 * b + 1, 0:D], mask[:, b, j, :], h1_lo[:, j, :], start=s, stop=False,
                       skip_group_check=True)
                    ins = mm(ps[:, 2 * b + 1, 0:DE], mask[:, b, j, :], h1_hi[:, j, 0:DE], start=False, stop=e,
                             skip_group_check=True)
                return ins

            def h2_transposes(t, b):
                pe.wait_ge(h2_hi_done, t + 1)
                pe.wait_ge(h2_lo_done, t + 1)
                for part, src in enumerate((h2_hi, h2_lo)):
                    for c in range(DC):
                        ins = nc.tensor.transpose(ps16(6)[:, (part * DC + c) * P:(part * DC + c + 1) * P],
                                                  src[:, b, c * P:(c + 1) * P], ident16[:, :])
                ins.then_inc(h2_t_ps, 1)

            def scores(t):
                pe.wait_ge(h2_t_done, t + 1)
                n = 0
                for ha, wb in ((0, wa_hi), (0, wa_lo), (1, wa_hi)):
                    for c in range(DC):
                        ins = mm(ps[:, 7, bass.ds(t * (2 * HEADS), 2 * HEADS)],
                                 h2_t[:, ha * DC + c, bass.ds(t * P, P)], wb[:, c, :], start=(n == 0),
                                 stop=(n == 5), skip_group_check=True)
                        n += 1
                ins.then_inc(sd_ps, 1)

            def layer1(i, first, last):
                for b in range(2):
                    for g in range(NB // TG):
                        if b == 0:
                            transpose_group(i, 1, g, False)
                        elif not last:
                            transpose_group(i + 1, 0, g, False)
                        ins = products1(i, b, g, first)
                        if g == NB // TG - 1:
                            ins.then_inc(l1_ps, 1)
                        if g == 2 and not (first and b == 0):
                            h2_transposes(2 * i + b - 1, 1 - b)
                        if g == 3 and not (first and b == 0):
                            if first:
                                pe.wait_ge(wa_done, 1)
                            scores(2 * i + b - 1)

            pe.wait_ge(deg_copied, 1)
            for b in range(2):
                for g in (2 * b, 2 * b + 1):
                    transpose_group(0, 0, g, True)
                layer0(NB // 2 - 1, False, (b,))
            layer1(0, True, False)
            with nc.tensor.Fori(1, NB // 2 - 1) as i:
                layer1(i, False, False)
            layer1(NB // 2 - 1, False, True)
            def ht_block(i, first):
                for b in range(2):
                    t = 2 * i + b
                    if first and b == 0:
                        pe.wait_ge(w2_lo_done, 1)
                    for half in range(2):
                        if not first:
                            pe.wait_ge(ht_lo_done, HEADS * (t - 2) + 2 * half + 2)
                        n = 0
                        for ha, wb in ((0, w2_hi), (0, w2_lo), (1, w2_hi)):
                            for c in range(DC):
                                ins = mm(ps[:, 2 * b + half, :], h2_t[:, ha * DC + c, bass.ds(t * P, P)],
                                         wb[:, c, 512 * half:512 * half + 512], start=(n == 0), stop=(n == 5))
                                n += 1
                        ins.then_inc(ht_ps, 1)

            pe.wait_ge(l1_taken, NB)
            ht_block(0, True)
            h2_transposes(NB - 1, 1)
            scores(NB - 1)
            pe.wait_ge(scaled_u, 1)
            nc.tensor.transpose(ps[0:HEADS * NB, 4, 0:P], up_i[:, :, :].rearrange("p t h -> p (t h)"),
                                ident[:, :]).then_inc(ut_ps, 1)
            with nc.tensor.Fori(1, NB // 2) as i:
                ht_block(i, False)

            def head_products(q, hp, b, first):
                head = 2 * hp + b
                group = q * HEADS + head
                for j in range(NB):
                    step = group * NB + j
                    if first and b == 0 and j == 0:
                        pe.wait_ge(ht_lo_done, HEADS * NB)
                        pe.wait_ge(ht_hi_done, HEADS * NB)
                        pe.wait_ge(ht_ones, 1)
                    pe.wait_ge(p_hi_done, step + 1)
                    pe.wait_ge(p_lo_done, step + 1)
                    s, e = (j == 0), (j == NB - 1)
                    slot = j % 4
                    for r in range(QB):
                        if j == 0 and not first:
                            pe.wait_ge(head_scaled, (group - 2) * QB + r + 1)
                        bank = 4 * b + r
                        hi = p_hi[:, slot, r * P:(r + 1) * P]
                        lo = p_lo[:, slot, r * P:(r + 1) * P]
                        mm(ps[:, bank, 0:DE], hi, ht_hi[:, head, j, 0:DE], start=s, stop=False)
                        mm(ps[:, bank, 0:DE], hi, ht_lo[:, head, j, 0:DE], start=False, stop=False)
                        ins = mm(ps[:, bank, 0:DE], lo, ht_hi[:, head, j, 0:DE], start=False, stop=e)
                    ins.then_inc(p_used, 1)

            def both_heads(q, hp, first):
                for b in range(2):
                    head_products(q, hp, b, first)

            both_heads(0, 0, True)
            both_heads(0, 1, False)
            with nc.tensor.Fori(1, NQ) as q:
                with nc.tensor.Fori(0, HEADS // 2) as hp:
                    both_heads(q, hp, False)

            def binary_product(i, first):
                for b in range(2):
                    t = 2 * i + b
                    pe.wait_ge(ba_done, t + 1)
                    if first and b == 0:
                        pe.wait_ge(head_scaled, NQ * HEADS * QB)
                    if not first:
                        pe.wait_ge(ba_t_done, t - 1)
                    for c in range(DC):
                        ins = nc.tensor.transpose(ps16(b)[:, c * P:(c + 1) * P],
                                                  ba[:, t, c * P:(c + 1) * P], ident16[:, :])
                    ins.then_inc(ba_t_ps, 1)
                for b in range(2):
                    t = 2 * i + b
                    pe.wait_ge(ba_t_done, t + 1)
                    if not first:
                        pe.wait_ge(xw_done, t - 1)
                    for c in range(DC):
                        ins = mm(ps[:, 2 + b, 0:D], ba_t[:, b, c, :], bw_t[:, c, :], start=(c == 0),
                                 stop=(c == DC - 1))
                    ins.then_inc(xw_ps, 1)

            binary_product(0, True)
            with nc.tensor.Fori(1, NB // 2) as i:
                binary_product(i, False)

            def layer3(i, first):
                for k in range(4):
                    pe.wait_ge(at3_in[k], 16 * (i + 1))
                    if not first:
                        pe.wait_ge(o_done, 4 * (i - 1) + k + 1)
                    for j in range(NB):
                        if first and k == 0:
                            pe.wait_ge(xw_done, j + 1)
                        mm(ps[:, 4 + k, 0:D], at3[:, k, 0, j, :], xw[:, j, :], start=(j == 0), stop=False)
                        ins = mm(ps[:, 4 + k, 0:D], at3[:, k, 1, j, :], xw[:, j, :], start=False,
                                 stop=(j == NB - 1))
                    ins.then_inc(o_ps, 1)

            layer3(0, True)
            with nc.tensor.Fori(1, NB // 4) as i:
                layer3(i, False)

        @block.scalar
        def _(act):
            copy = ACT.Copy

            act.wait_ge(w0_in, 48)
            nc.scalar.activation(w0_hi, w0_f, copy, scale=W_SCALE).then_inc(w0_hi_done, 1)
            act.wait_ge(w3_t_ps, 1)
            nc.scalar.activation(bw_t[:, :, :].rearrange("p c d -> p (c d)"), ps16(0)[:, 0:DC * D], copy
                                 ).then_inc(w3_t_done, 1)

            def adj_high(j, s, k, need):
                act.wait_ge(half_in[k], need)
                nc.scalar.activation(nat[:, s * HBK:(s + 1) * HBK, 0, j, :],
                                     stage[:, k, :].rearrange("p (a n) -> p a n", a=HBK), copy,
                                     scale=ADJ_SCALE).then_inc(nat_hi_done, 1)

            def h0_turned(t, b, first):
                act.wait_ge(h0_t_ps, t + 1)
                if not first:
                    act.wait_ge(hw_ps, t - 1)
                nc.scalar.activation(h0_t[:, b, :, :].rearrange("p a n -> p (a n)"),
                                     ps16(b)[:, 0:2 * DC * P], copy).then_inc(h0_t_done, 1)

            def hw_copy(t, b):
                act.wait_ge(hw_ps, t + 1)
                nc.scalar.activation(hw[:, t, :], ps[:, 2 + b, 0:D], copy,
                                     scale=1.0 / (H_SCALE * W_SCALE)).then_inc(hw_done, 1)

            def load_step(i, first, last):
                for b in range(2):
                    t = 2 * i + b
                    adj_high(t, 0, 2 * b, 16 * (i + 1))
                    adj_high(t, 1, 2 * b + 1, 16 * (i + 1))
                    if not (last and b == 1):
                        h0_turned(t + 1, 1 - b, first and b == 0)
                    if not (first and b == 0):
                        hw_copy(t - 1, 1 - b)

            h0_turned(0, 0, True)
            load_step(0, True, False)
            with nc.scalar.Fori(1, NB // 2 - 1) as i:
                load_step(i, False, False)
            load_step(NB // 2 - 1, False, True)
            hw_copy(NB - 1, 1)

            act.wait_ge(dinv_scaled, 2)
            act.wait_ge(hw_done, NB)
            act.wait_ge(hw_ps, NB)
            with nc.scalar.Fori(0, NB) as t:
                nc.scalar.activation(g_hi[:, t, :], hw[:, t, :], copy,
                                     scale=dinv_in[:, bass.ds(t, 1)]).then_inc(g_hi_done, 1)

            def h1_high(i, b):
                act.wait_ge(relu1, 2 * i + b + 1)
                act.wait_ge(rs1, 2 * i + b + 1)
                nc.scalar.activation(h1_hi[:, 2 * i + b, 0:D], ln_relu[:, b, :], copy,
                                     scale=rstd[:, bass.ds(2 * i + b, 1)]).then_inc(h1_hi_done, 1)

            with nc.scalar.Fori(0, NB // 2 - 1) as i:
                for b in range(2):
                    h1_high(i, b)

            def adj_t_group(i, b, g, first):
                n = 4 * (2 * i + b) + g
                act.wait_ge(t_ps, n + 1)
                if g == 0 and not first:
                    act.wait_ge(l1_ps, 2 * i + b - 1)
                    act.wait_ge(at_sent[b], 16 * i)
                    act.wait_ge(e_sent[b], 16 * i)
                nc.scalar.activation(at[:, b, 0, TG * g:TG * g + TG, :].rearrange("p j n -> p (j n)"),
                                     ps[:, 4 + g % 2, :], copy, scale=ADJ_SCALE).then_inc(at_hi_done, 1)
                nc.scalar.activation(e_out[:, b, TG * g:TG * g + TG, :].rearrange("p j n -> p (j n)"),
                                     ps[:, 4 + g % 2, :], ACT.Exp, bias=amax[:, 2:3]).then_inc(e_done, 1)

            def h2_high(t, b):
                act.wait_ge(relu2, t + 1)
                act.wait_ge(rs2, t + 1)
                nc.scalar.activation(h2_hi[:, b, :], ln_relu[:, b, :], copy,
                                     scale=row_n[:, b, 7:8]).then_inc(h2_hi_done, 1)

            def h2_turned(t):
                act.wait_ge(h2_t_ps, t + 1)
                nc.scalar.activation(h2_t[:, :, bass.ds(t * P, P)],
                                     ps16(6)[:, 0:2 * DC * P].rearrange("p (a n) -> p a n", a=2 * DC), copy
                                     ).then_inc(h2_t_done, 1)

            act.wait_ge(amax_neg, 1)
            act.wait_ge(y_ps, NB - 3)
            for b in range(2):
                for g in (2 * b, 2 * b + 1):
                    adj_t_group(0, 0, g, True)
                h1_high(NB // 2 - 1, b)
            for g in range(NB // TG):
                adj_t_group(0, 1, g, True)
            act.wait_ge(w2_in, 32)
            act.wait_ge(y_ps, NB)
            nc.scalar.activation(w2_hi, w2_f, copy, scale=W_SCALE).then_inc(w2_hi_done, 1)

            def layer1(i):
                for b in range(2):
                    for g in range(NB // TG):
                        adj_t_group(i, b, g, False)
                        if g == 1:
                            h2_high(2 * i + b - 2, b)
                        if g == 2:
                            h2_turned(2 * i + b - 2)

            with nc.scalar.Fori(1, NB // 2) as i:
                layer1(i)
            for b in range(2):
                h2_high(NB - 2 + b, b)
                h2_turned(NB - 2 + b)

            act.wait_ge(d_shift, 1)
            flat = "p t h -> p (t h)"
            nc.scalar.activation(vp_j[:, :, :].rearrange(flat), w_j[:, :, :].rearrange(flat), ACT.Exp,
                                 scale=SLOPE).then_inc(exps, 1)
            act.wait_ge(exps, 1)
            nc.scalar.activation(w_j[:, :, :].rearrange(flat), w_j[:, :, :].rearrange(flat), ACT.Exp,
                                 scale=1.0 - SLOPE).then_inc(exps, 1)
            act.wait_ge(up_arg, 1)
            nc.scalar.activation(up_i[:, :, :].rearrange(flat), up_i[:, :, :].rearrange(flat), ACT.Exp,
                                 scale=-(1.0 - SLOPE)).then_inc(exps, 1)

            def ht_high(i):
                for b in range(2):
                    t = 2 * i + b
                    for h in range(HEADS):
                        act.wait_ge(ht_ps, 2 * t + h // 2 + 1)
                        nc.scalar.activation(ht_hi[:, h, t, 0:D],
                                             ps[:, 2 * b + h // 2, (h % 2) * D:(h % 2 + 1) * D], copy,
                                             scale=vp_j[:, t, h:h + 1]).then_inc(ht_hi_done, 1)

            act.wait_ge(exps, 3)
            for b in range(2):
                act.wait_ge(at_sent[b], 16 * NB // 2)
                act.wait_ge(e_sent[b], 16 * NB // 2)
            ht_high(0)
            act.wait_ge(ut_ps, 1)
            nc.scalar.activation(up_t[0:HEADS * NB, :], ps[0:HEADS * NB, 4, 0:P], copy).then_inc(ut_done, 1)
            with nc.scalar.Fori(1, NB // 2) as i:
                ht_high(i)

            def scale_head(group, b, r, early):
                if r == 0:
                    act.wait_ge(inv_done, group + 1)
                if not (early and r < 2):
                    act.wait_ge(head_added, group * QB + r - 1)
                nc.scalar.activation(head_out[:, r % 2, :], ps[:, 4 * b + r, 0:D], copy,
                                     scale=inv_l[:, b, r:r + 1]).then_inc(head_scaled, 1)

            def hold(r, k):
                nc.scalar.activation(held_act[:, 2 * r + k:2 * r + k + 1], neg_half[:, 0:1], copy)

            def binary_input(part, q, r):
                t = QB * q + r
                n = 3 * t
                if part == 1:
                    act.wait_ge(head_added, (q + 1) * (HEADS * QB) - QB + r + 1)
                    nc.scalar.activation(ba[:, t, :], x[:, t, :], copy, scale=-1.0 / D,
                                         accum_out=neg_mean[:, r:r + 1]).then_inc(ba_chain, 1)
                elif part == 2:
                    act.wait_ge(ba_chain, 2 * t + 1)
                    hold(r, 0)
                    nc.scalar.activation(ba[:, t, :], x[:, t, :], ACT.Sign, bias=neg_mean[:, r:r + 1]
                                         ).then_inc(ba_chain, 1)
                else:
                    act.wait_ge(ba_chain, 2 * t + 2)
                    hold(r, 1)
                    nc.scalar.activation(ba[:, t, :], ba[:, t, :], ACT.Relu).then_inc(ba_done, 1)

            def head_high(q, hp, b, first, second, norms=False):
                head = 2 * hp + b
                group = q * HEADS + head
                for j in range(NB):
                    step = group * NB + j
                    act.wait_ge(p_done, step + 1)
                    if not (first and j < 4):
                        act.wait_ge(p_used, step - 3)
                    nc.scalar.activation(p_hi[:, j % 4, :], prob[:, j % 4, :], copy).then_inc(p_hi_done, 1)
                    if not first and 4 <= j < 4 + QB:
                        scale_head(group - 1, 1 - b, j - 4, second)
                    if norms and j >= 8:
                        for part in ((1,) if j % 2 == 0 else (2, 3)):
                            binary_input(part, q - 1, (j - 8) // 2)

            head_high(0, 0, 0, True, False)
            head_high(0, 0, 1, False, True)
            for b in range(2):
                head_high(0, 1, b, False, False)
            with nc.scalar.Fori(1, NQ) as q:
                for hp in range(HEADS // 2):
                    for b in range(2):
                        head_high(q, hp, b, False, False, norms=(hp == 0 and b == 0))
            for r in range(QB):
                scale_head(NQ * HEADS - 1, 1, r, False)
            for r in range(QB):
                for part in (1, 2, 3):
                    binary_input(part, NQ - 1, r)

            def binary_copies(i, first):
                for b in range(2):
                    t = 2 * i + b
                    act.wait_ge(ba_t_ps, t + 1)
                    if not first:
                        act.wait_ge(xw_ps, t - 1)
                    nc.scalar.activation(ba_t[:, b, :, :].rearrange("p c n -> p (c n)"), ps16(b)[:, 0:DC * P],
                                         copy).then_inc(ba_t_done, 1)
                for b in range(2):
                    t = 2 * i + b
                    act.wait_ge(xw_ps, t + 1)
                    nc.scalar.activation(xw[:, t, :], ps[:, 2 + b, 0:D], copy, scale=1.0 / ADJ_SCALE
                                         ).then_inc(xw_done, 1)

            binary_copies(0, True)
            with nc.scalar.Fori(1, NB // 2) as i:
                binary_copies(i, False)

        @block.vector
        def _(dve):
            v = nc.vector
            made = [0]

            def hold(k):
                v.memset(held[:, k:k + 1], 0.0)

            def link(ins):
                made[0] += 1
                ins.then_inc(dv, 1)
                dve.wait_ge(dv, made[0])

            dve.wait_ge(w0_in, 48)
            v.tensor_scalar(w3_s, w3_f, 0.0, None, ALU.is_lt).then_inc(dv, 1)
            made[0] += 1
            dve.wait_ge(dv, made[0])
            v.scalar_tensor_tensor(w3_s, w3_f, 0.0, w3_s, ALU.is_gt, ALU.subtract).then_inc(w3_signed, 1)
            dve.wait_ge(w0_hi_done, 1)
            v.scalar_tensor_tensor(w0_lo, w0_f, W_SCALE, w0_hi, ALU.mult, ALU.subtract).then_inc(w0_lo_done, 1)

            dve.wait_ge(x_in, 16)
            for t in range(NB):
                ins = v.bn_stats(stats[:, t, :], x[:, t, :])
            link(ins)
            for t in range(NB):
                ins = v.bn_aggr(mean_var[:, t, :], stats[:, t, :])
            link(ins)
            v.tensor_scalar(var_eps[:, :], mean_var[:, :, 1], LN_EPS, H_SCALE ** -2, ALU.add, ALU.mult
                            ).then_inc(stats_done, 1)

            def adj_low(j, s, k, n):
                dve.wait_ge(nat_hi_done, n + 1)
                v.scalar_tensor_tensor(nat[:, s * HBK:(s + 1) * HBK, 1, j, :],
                                       stage[:, k, :].rearrange("p (a n) -> p a n", a=HBK), ADJ_SCALE,
                                       nat[:, s * HBK:(s + 1) * HBK, 0, j, :], ALU.mult, ALU.subtract
                                       ).then_inc(nat_lo_done, 1)

            def relu_shift(t, b):
                v.tensor_scalar(hrelu[:, b, :], x[:, t, :], mean_var[:, t, 0:1], 0.0, ALU.subtract, ALU.max
                                ).then_inc(relu0, 1)

            def h0_parts(t, b, first):
                dve.wait_ge(relu0, t + 1)
                if not first:
                    dve.wait_ge(h0_t_ps, t - 1)
                v.tensor_scalar(hn_hi[:, b, :], hrelu[:, b, :], rstd[:, bass.ds(t, 1)], None, ALU.mult
                                ).then_inc(h0_hi_done, 1)
                dve.wait_ge(h0_hi_done, t + 1)
                v.scalar_tensor_tensor(hn_lo[:, b, :], hrelu[:, b, :], rstd[:, bass.ds(t, 1)], hn_hi[:, b, :],
                                       ALU.mult, ALU.subtract).then_inc(h0_lo_done, 1)

            def load_step(i, left):
                for b in range(2):
                    t = 2 * i + b
                    adj_low(t, 0, 2 * b, 2 * t)
                    adj_low(t, 1, 2 * b + 1, 2 * t + 1)
                    if left >= 2:
                        h0_parts(t + 2, b, False)
                    if left >= 4:
                        dve.wait_ge(h0_lo_done, t + 3)
                        relu_shift(t + 4, b)

            for b in range(2):
                relu_shift(b, b)
            dve.wait_ge(rstd_done, 1)
            for b in range(2):
                h0_parts(b, b, True)
            dve.wait_ge(h0_lo_done, 2)
            for b in range(2):
                relu_shift(2 + b, b)
            with nc.vector.Fori(0, NB // 2 - 2) as i:
                load_step(i, 4)
            load_step(NB // 2 - 2, 2)
            load_step(NB // 2 - 1, 0)

            dve.wait_ge(deg_done, 1)
            for t in range(NB):
                ins = v.tensor_tensor_reduce(junk[:, t % JUNK, :], ps[:, 4 + t // 4, (t % 4) * P:(t % 4 + 1) * P],
                                             ident[:, :], 1.0, 0.0, ALU.mult, ALU.add, deg[:, t:t + 1])
                if t == JUNK - 1:
                    link(ins)
            ins.then_inc(deg_copied, 1)
            dve.wait_ge(dinv_done, 1)
            v.tensor_scalar(dinv_in[:, :], dinv[:, :], 256.0, None, ALU.mult).then_inc(dinv_scaled, 1)
            v.tensor_scalar(dinv_out[:, :], dinv[:, :], 1.0 / 256.0, None, ALU.mult).then_inc(dinv_scaled, 1)
            dve.wait_ge(dinv_scaled, 2)
            dve.wait_ge(hw_done, NB)
            with nc.vector.Fori(0, NB) as t:
                dve.wait_ge(g_hi_done, t + 1)
                v.scalar_tensor_tensor(g_lo[:, t, :], hw[:, t, :], dinv_in[:, bass.ds(t, 1)], g_hi[:, t, :],
                                       ALU.mult, ALU.subtract).then_inc(g_lo_done, 1)
            dve.wait_ge(g_lo_done, NB)
            v.memset(h1_hi[:, :, D:DE], 1.0).then_inc(ones_col, 1)
            v.memset(nat_max, 0.0).then_inc(max_made, 1)

            CHAIN0 = 3

            def h1_low(t, b):
                dve.wait_ge(h1_hi_done, t + 1)
                v.scalar_tensor_tensor(h1_lo[:, t, :], ln_relu[:, b, :], rstd[:, bass.ds(t, 1)],
                                       h1_hi[:, t, 0:D], ALU.mult, ALU.subtract).then_inc(h1_lo_done, 1)

            def layer0(t, b, maxima, first=False):
                if maxima:
                    for m in range(2):
                        dve.wait_ge(max_made, 2 * t + m + 1)
                        v.tensor_tensor(nat_max, nat_max,
                                        nat[:, 2 * t + m, 0, :, :].rearrange("p a n -> p (a n)"), ALU.max
                                        ).then_inc(max_made, 1)
                v.tensor_tensor(x[:, t, :], x[:, t, :], bias, ALU.add).then_inc(dl, 1)
                dve.wait_ge(dl, CHAIN0 * t + 1)
                dve.wait_ge(y_ps, t + 1)
                v.scalar_tensor_tensor(x[:, t, :], ps[:, b, 0:D], dinv_out[:, bass.ds(t, 1)], x[:, t, :],
                                       ALU.mult, ALU.add).then_inc(y_taken, 1)
                if not first:
                    h1_low(t - 1, 1 - b)
                dve.wait_ge(y_taken, t + 1)
                hold(0 + 2 * (b % 2))
                v.bn_stats(stats[:, b, :], x[:, t, :]).then_inc(dl, 1)
                dve.wait_ge(dl, CHAIN0 * t + 2)
                hold(1 + 2 * (b % 2))
                v.bn_aggr(mean_var[:, b, :], stats[:, b, :]).then_inc(dl, 1)
                dve.wait_ge(dl, CHAIN0 * t + 3)
                v.tensor_scalar(var_eps[:, bass.ds(t, 1)], mean_var[:, b, 1:2], LN_EPS, H_SCALE ** -2,
                                ALU.add, ALU.mult).then_inc(ve1, 1)
                v.tensor_scalar(ln_relu[:, b, :], x[:, t, :], mean_var[:, b, 0:1], 0.0, ALU.subtract,
                                ALU.max).then_inc(relu1, 1)

            def w2_a(c):
                for h in range(HEADS):
                    for side in range(2):
                        k = side * HEADS + h
                        link(v.tensor_tensor_reduce(wa_junk, w2_f[:, c, h * D:(h + 1) * D],
                                                    a_bc[:, (2 * h + side) * D:(2 * h + side + 1) * D],
                                                    W_SCALE, 0.0, ALU.mult, ALU.add, wa[:, c, k:k + 1]))

            layer0(0, 0, True, True)
            layer0(1, 1, True)
            with nc.vector.Fori(1, NB // 4) as i:
                for b in range(2):
                    layer0(2 * i + b, b, True)
            dve.wait_ge(max_made, NB + 1)
            v.tensor_reduce(amax[:, 0:1], nat_max, AX_X, ALU.max).then_inc(amax_part, 1)
            with nc.vector.Fori(NB // 4, NB // 2 - 2) as i:
                for b in range(2):
                    layer0(2 * i + b, b, False)
            dve.wait_ge(w2_in, 32)
            for b in range(2):
                layer0(NB - 4 + b, b, False)
                w2_a(b)
            link(v.tensor_copy(wa_hi[:, :, :], wa[:, :, :]))
            v.tensor_tensor(wa_lo[:, :, :], wa[:, :, :], wa_hi[:, :, :], ALU.subtract).then_inc(wa_done, 1)
            dve.wait_ge(amax_all, 1)
            v.tensor_scalar(amax[:, 2:3], amax[:, 1:2], -1.0 / ADJ_SCALE, None, ALU.mult).then_inc(amax_neg, 1)

            def adj_t_group(i, b, g):
                n = 4 * (2 * i + b) + g
                dve.wait_ge(e_done, n + 1)
                v.scalar_tensor_tensor(at[:, b, 1, TG * g:TG * g + TG, :].rearrange("p j n -> p (j n)"),
                                       ps[:, 4 + g % 2, :], ADJ_SCALE,
                                       at[:, b, 0, TG * g:TG * g + TG, :].rearrange("p j n -> p (j n)"),
                                       ALU.mult, ALU.subtract).then_inc(at_lo_done, 1)
                v.tensor_scalar(mask[:, b, TG * g:TG * g + TG, :].rearrange("p j n -> p (j n)"),
                                ps[:, 4 + g % 2, :], 0.0, None, ALU.is_gt).then_inc(mask_done, 1)

            for b in range(2):
                for g in (2 * b, 2 * b + 1):
                    adj_t_group(0, 0, g)
                layer0(NB - 2 + b, b, False)
            h1_low(NB - 1, 1)

            CHAIN1 = 8

            def row_block(t, b):
                rn = row_n[:, b, :]
                base = CHAIN1 * t

                def after(k, ins):
                    ins.then_inc(dm, 1)
                    dve.wait_ge(dm, base + k)

                dve.wait_ge(l1_ps, t + 1)
                v.tensor_scalar(rn[:, 0:1], ps[:, 2 * b + 1, D:DE], NORM_EPS ** 2, None, ALU.max
                                ).then_inc(n_done, 1)
                v.tensor_scalar(rn[:, 2:3], ps[:, 2 * b, D:DE], 1.0 / ADJ_SCALE, None, ALU.mult).then_inc(dm, 1)
                dve.wait_ge(dm, base + 1)
                dve.wait_ge(c_done, t + 1)
                after(2, v.scalar_tensor_tensor(rn[:, 3:4], ps[:, 2 * b + 1, D:DE], rn[:, 1:2], rn[:, 2:3],
                                                ALU.mult, ALU.add))
                after(3, v.reciprocal(rn[:, 4:5], rn[:, 3:4]))
                v.tensor_scalar(rn[:, 5:6], rn[:, 1:2], rn[:, 4:5], 1.0 / H_SCALE, ALU.mult, ALU.mult
                                ).then_inc(dm, 1)
                after(5, v.tensor_scalar(rn[:, 8:9], rn[:, 4:5], 1.0 / (H_SCALE * ADJ_SCALE), None, ALU.mult))
                after(6, v.scalar_tensor_tensor(x[:, t, :], ps[:, 2 * b, 0:D], rn[:, 8:9], x[:, t, :],
                                                ALU.mult, ALU.add))
                v.scalar_tensor_tensor(x[:, t, :], ps[:, 2 * b + 1, 0:D], rn[:, 5:6], x[:, t, :],
                                       ALU.mult, ALU.add).then_inc(l1_taken, 1)
                dve.wait_ge(l1_taken, t + 1)
                hold(0 + 2 * (b % 2))
                after(7, v.bn_stats(stats[:, b, :], x[:, t, :]))
                hold(1 + 2 * (b % 2))
                after(8, v.bn_aggr(mean_var[:, b, :], stats[:, b, :]))
                v.tensor_scalar(rn[:, 6:7], mean_var[:, b, 1:2], LN_EPS, H_SCALE ** -2, ALU.add, ALU.mult
                                ).then_inc(ve2, 1)
                v.tensor_scalar(ln_relu[:, b, :], x[:, t, :], mean_var[:, b, 0:1], 0.0, ALU.subtract, ALU.max
                                ).then_inc(relu2, 1)

            def h2_low(t, b):
                dve.wait_ge(h2_hi_done, t + 1)
                v.scalar_tensor_tensor(h2_lo[:, b, :], ln_relu[:, b, :], row_n[:, b, 7:8], h2_hi[:, b, :],
                                       ALU.mult, ALU.subtract).then_inc(h2_lo_done, 1)

            def layer1(i, b, low):
                adj_t_group(i, b, 0)
                if low:
                    row_block(2 * i + b - 2, b)
                adj_t_group(i, b, 1)
                if low:
                    h2_low(2 * i + b - 2, b)
                adj_t_group(i, b, 2)
                adj_t_group(i, b, 3)

            layer1(0, 1, False)
            dve.wait_ge(w2_hi_done, 1)
            v.scalar_tensor_tensor(w2_lo, w2_f, W_SCALE, w2_hi, ALU.mult, ALU.subtract).then_inc(w2_lo_done, 1)
            with nc.vector.Fori(1, NB // 2) as i:
                for b in range(2):
                    layer1(i, b, True)
            for b in range(2):
                row_block(NB - 2 + b, b)
                h2_low(NB - 2 + b, b)

            dve.wait_ge(sd_ps, NB)
            link(v.tensor_scalar(sd[:, :, :].rearrange("p t k -> p (t k)"), ps[:, 7, 0:2 * HEADS * NB],
                                 1.0 / (H_SCALE * W_SCALE), None, ALU.mult))
            v.tensor_reduce(dmax[:, 0, :], sd[:, :, HEADS:2 * HEADS].rearrange("p t h -> p h t"), AX_X, ALU.max
                            ).then_inc(dmax_part, 1)
            dve.wait_ge(dmax_all, 1)
            dmax_bc = dmax[:, 1:2, :].broadcast_to([P, NB, HEADS])
            v.tensor_tensor(w_j[:, :, :], sd[:, :, HEADS:2 * HEADS], dmax_bc, ALU.subtract).then_inc(d_shift, 1)
            link(v.tensor_tensor(up_i[:, :, :], sd[:, :, 0:HEADS], dmax_bc, ALU.add))
            v.tensor_scalar(up_i[:, :, :], up_i[:, :, :], 0.0, None, ALU.max).then_inc(up_arg, 1)
            dve.wait_ge(exps, 3)
            v.tensor_scalar(up_i[:, :, :], up_i[:, :, :], P_SCALE, None, ALU.mult).then_inc(scaled_u, 1)
            v.tensor_scalar(w_j[:, :, :], w_j[:, :, :], P_SCALE, None, ALU.mult).then_inc(scaled_w, 1)
            for b in range(2):
                dve.wait_ge(at_sent[b], 16 * NB // 2)
                dve.wait_ge(e_sent[b], 16 * NB // 2)
            vp_cols = vp_j[:, :, :].rearrange("p t h -> p h t")
            link(v.tensor_scalar(ht_hi[:, :, :, D], vp_cols, H_SCALE * W_SCALE, None, ALU.mult))
            v.scalar_tensor_tensor(ht_lo[:, :, :, D], vp_cols, H_SCALE * W_SCALE, ht_hi[:, :, :, D],
                                   ALU.mult, ALU.subtract).then_inc(ht_ones, 1)
            with nc.vector.Fori(0, NB // 2) as i:
                for b in range(2):
                    for h in range(HEADS):
                        n = HEADS * (2 * i + b) + h
                        if h % 2 == 0:
                            dve.wait_ge(ht_hi_done, n + 2)
                        v.scalar_tensor_tensor(ht_lo[:, h, 2 * i + b, 0:D],
                                               ps[:, 2 * b + h // 2, (h % 2) * D:(h % 2 + 1) * D],
                                               vp_j[:, 2 * i + b, h:h + 1], ht_hi[:, h, 2 * i + b, 0:D],
                                               ALU.mult, ALU.subtract).then_inc(ht_lo_done, 1)

            def numerators(q, h, j, step):
                if h == 0 and j % TG == 0:
                    dve.wait_ge(e_loaded[j // TG], 16 * TG * (q + 1))
                v.scalar_tensor_tensor(prob[:, j % 4, :], u_bc[:, h, bass.ds(q * (QB * P), QB * P)],
                                       w_j[:, j, h:h + 1], e_in[:, j, :], ALU.max, ALU.mult).then_inc(p_done, 1)

            def low_part(j, step):
                dve.wait_ge(p_hi_done, step + 1)
                v.tensor_tensor(p_lo[:, j % 4, :], prob[:, j % 4, :], p_hi[:, j % 4, :], ALU.subtract
                                ).then_inc(p_lo_done, 1)

            def head_inverse(group, b):
                dve.wait_ge(p_used, (group + 1) * NB)
                v.tensor_scalar(inv_l[:, b, :], ps[:, 4 * b:4 * b + QB, D], float(HEADS), None, ALU.mult
                                ).then_inc(sum4, 1)
                dve.wait_ge(sum4, group + 1)
                v.reciprocal(inv_l[:, b, :], inv_l[:, b, :]).then_inc(inv_done, 1)

            def quarter(q, first):
                for h in range(HEADS):
                    group = q * HEADS + h
                    if first:
                        dve.wait_ge(u_in[h], 16)
                    for j in range(NB):
                        step = group * NB + j
                        if j == 4 and not (first and h == 0):
                            head_inverse(group - 1, (h + 1) % 2)
                        numerators(q, h, j, step)
                        if not (first and h == 0 and j == 0):
                            low_part((j - 1) % NB, step - 1)

            quarter(0, True)
            with nc.vector.Fori(1, NQ) as q:
                quarter(q, False)
            low_part(NB - 1, NQ * HEADS * NB - 1)
            head_inverse(NQ * HEADS - 1, 1)

            with nc.vector.Fori(0, NB // 4) as i:
                for k in range(4):
                    dve.wait_ge(o_ps, 4 * i + k + 1)
                    v.scalar_tensor_tensor(x[:, 4 * i + k, :], ps[:, 4 + k, 0:D], 0.0, x[:, 4 * i + k, :],
                                           ALU.max, ALU.add).then_inc(o_done, 1)


_INS = ["x", "adj", "L0_gnn_weight", "L0_gnn_bias", "L2_gnn_W", "L2_gnn_a", "L3_gnn_weight"]
_OUT = ((2048, 256), "float32")


def kernel(**inputs):
    import numpy as _np
    import concourse.bacc as _bacc
    from concourse import mybir as _mybir
    from concourse.bass_utils import run_bass_kernel_spmd as _run

    nc = _bacc.Bacc("TRN2", target_bir_lowering=False, num_devices=1)
    arrays, args = {}, []
    for name in _INS:
        a = _np.ascontiguousarray(inputs[name])
        arrays[f"in_{name}_dram"] = a
        args.append(nc.dram_tensor(f"in_{name}_dram", a.shape, _mybir.dt.from_np(a.dtype),
                                   kind="ExternalInput").ap())
    args.append(nc.dram_tensor("out_dram", _OUT[0], _mybir.dt.from_np(_np.dtype(_OUT[1])),
                               kind="ExternalOutput").ap())
    gnn_stack(nc, *args)
    r = _run(nc, [arrays], core_ids=[0])
    return r.results[0]["out_dram"]
```

```python
from contextlib import ExitStack

import concourse.bass as bass
from concourse import mybir

F32 = mybir.dt.float32
F16 = mybir.dt.float16
ALU = mybir.AluOpType
ACT = mybir.ActivationFunctionType
AX_X = mybir.AxisListType.X
RMAX = bass.bass_isa.ReduceOp.max

P = 128
KB = 1024
ADJ_SCALE = 256.0
H_SCALE = 16.0
W_SCALE = 16.0
P_SCALE = 4096.0
LN_EPS = 1e-5
NORM_EPS = 1e-12
SLOPE = 0.01


def gnn_stack(nc, x_d, adj_d, w0_d, b0_d, w2_d, a2_d, w3_d, out_d):
    N, D = x_d.shape
    NB = N // P
    DC = D // P
    HEADS = a2_d.shape[0]
    HD = HEADS * D
    DE = D + 1
    DS = D + 2
    QB = 4
    NQ = NB // QB
    HALF = N // 2
    HBK = NB // 2
    TG = 4

    x_rows = x_d.rearrange("(t p) d -> p t d", p=P)
    out_rows = out_d.rearrange("(t p) d -> t p d", p=P)
    adj_rows = adj_d.rearrange("(t p) n -> t p n", p=P)

    at_dram = nc.dram_tensor("adj_t_parts", (NB, P, 2 * N), F16, kind="Internal").ap()
    e_dram = nc.dram_tensor("exp_adj_t", (NB, NB, P, P), F32, kind="Internal").ap()
    u_dram = nc.dram_tensor("u_rows", (NB, HEADS, P), F32, kind="Internal").ap()

    with ExitStack() as ctx:
        def sb(name, shape, dt):
            return ctx.enter_context(nc.sbuf_tensor(name, shape, dt))

        def sem(name):
            return ctx.enter_context(nc.semaphore(name))

        x = sb("x", [P, NB, D], F32)
        ident = sb("ident", [P, P], F32)
        ident16 = sb("ident16", [P, P], F16)
        ones16 = sb("ones16", [P, P], F16)
        row_pair = sb("row_pair", [P, 2, D], F32)
        bias = row_pair[:, 0, :]
        head_out = row_pair
        bw_t = sb("bw_t", [P, DC, D], F16)
        neg_half = sb("neg_half", [P, NB], F32)
        stats = sb("stats", [P, NB, 6], F32)
        mean_var = sb("mean_var", [P, NB, 2], F32)
        var_eps = sb("var_eps", [P, NB], F32)
        rstd = sb("rstd", [P, NB], F32)
        deg = sb("deg", [P, NB], F32)
        dinv = sb("dinv", [P, NB], F32)
        dinv_in = sb("dinv_in", [P, NB], F32)
        dinv_out = sb("dinv_out", [P, NB], F32)
        wa_hi = sb("wa_hi", [P, DC, 2 * HEADS], F16)
        wa_lo = sb("wa_lo", [P, DC, 2 * HEADS], F16)
        wa = sb("wa", [P, DC, 2 * HEADS], F32)
        amax = sb("amax", [P, 4], F32)
        row_n = sb("row_n", [P, 2, 10], F32)
        held_act = sb("held_act", [P, 2 * QB], F32)
        held = sb("held", [P, 4], F32)
        sd = sb("sd", [P, NB, 2 * HEADS], F32)
        dmax = sb("dmax", [P, 3, HEADS], F32)
        w_j = sb("w_j", [P, NB, HEADS], F32)
        vp_j = sb("vp_j", [P, NB, HEADS], F32)
        up_i = sb("up_i", [P, NB, HEADS], F32)
        neg_mean = sb("neg_mean", [P, QB], F32)
        inv_l = sb("inv_l", [P, 2, QB], F32)

        ARENA = 184 * KB + 512
        arena = sb("arena", [P, ARENA // 4], F32)

        def view(off, shape, dt):
            size = 4 if dt == F32 else 2
            n = 1
            for s in shape:
                n *= s
            words = (n * size + 3) // 4
            v = arena[:, off // 4:off // 4 + words]
            if dt == F16:
                v = v.bitcast(F16)
            if len(shape) == 1:
                return v
            names = " ".join("abcd"[:len(shape)])
            return v.rearrange(f"p ({names}) -> p {names}", **{"abcd"[k]: s for k, s in enumerate(shape)})

        nat = view(0, [NB, 2, NB, P], F16)
        G0 = 128 * KB
        g_hi = view(G0, [NB, D], F16)
        g_lo = view(G0 + 8 * KB, [NB, D], F16)
        w0_f = view(G0, [DC, D], F32)
        w0_hi = view(G0 + 2 * KB, [DC, D], F16)
        w0_lo = view(G0 + 3 * KB, [DC, D], F16)
        w3_f = view(G0 + 4 * KB, [DC, D], F32)
        w3_s = view(G0 + 6 * KB, [DC, D], F16)
        hrelu = view(G0 + 8 * KB, [2, D], F32)
        hn_hi = view(G0 + 10 * KB, [2, D], F16)
        hn_lo = view(G0 + 11 * KB, [2, D], F16)
        h0_t = view(G0 + 12 * KB, [2, 2 * DC, P], F16)
        H1 = 144 * KB
        hw = view(H1, [NB, D], F32)
        h1_hi = view(H1, [NB, DS], F16)
        h1_lo = view(H1 + NB * DS * 2, [NB, D], F16)
        STG = 162 * KB
        stage = view(STG, [4, HALF], F32)
        LN = 178 * KB
        ln_relu = view(LN, [2, D], F32)
        nat_max = view(LN + 2 * KB, [N], F16)
        JUNK = 12
        junk = view(LN, [JUNK, P], F32)
        HT = HEADS * NB * DS * 2
        H2T = 2 * HT + 48 * KB
        at = view(0, [2, 2, NB, P], F16)
        mask = view(16 * KB, [2, NB, P], F16)
        e_out = view(24 * KB, [2, NB, P], F32)
        w2_f = view(56 * KB, [DC, HD], F32)
        a_bc = view(64 * KB, [HEADS * 2 * D], F32)
        wa_junk = view(72 * KB, [D], F32)
        h2_hi = view(74 * KB, [2, D], F16)
        h2_lo = view(75 * KB, [2, D], F16)
        h2_t = view(H2T, [2 * DC, N], F16)
        w2_hi = view(H2T + 16 * KB, [DC, HD], F16)
        w2_lo = view(H2T + 20 * KB, [DC, HD], F16)
        ht_hi = view(0, [HEADS, NB, DS], F16)
        ht_lo = view(HT, [HEADS, NB, DS], F16)
        PR = 2 * HT
        prob = view(PR, [4, QB * P], F32)
        p_hi = view(PR + 8 * KB, [4, QB * P], F16)
        p_lo = view(PR + 12 * KB, [4, QB * P], F16)
        U = PR + 16 * KB
        u_bc = view(U, [HEADS, N], F32)
        RING3 = U + 32 * KB
        at3 = view(RING3, [4, 2, NB, P], F16)
        ba_loop = view(RING3 + 24 * KB, [QB, D], F16)
        bat_loop = view(RING3 + 26 * KB, [2, 2 * DC, P], F16)
        ba_tail = view(RING3 + 40 * KB, [QB, D], F16)
        bat_tail = view(RING3 + 42 * KB, [2, 2 * DC, P], F16)
        xw = view(RING3 + 32 * KB, [NB, D], F16)
        up_t = view(RING3 + 32 * KB, [P], F32)
        e_in = view(RING3 + 40 * KB, [NB, QB * P], F32)

        EARLY = 4

        ps = ctx.enter_context(nc.psum_tensor("ps", [P, 8, 512], F32))

        def ps16(bank):
            return ps[:, bank, :].bitcast(F16)

        x_in = sem("x_in")
        w0_in = sem("w0_in")
        w2_in = sem("w2_in")
        consts = sem("consts")
        ident_zero = sem("ident_zero")
        half_in = [sem(f"half_in{k}") for k in range(4)]
        nat_hi_done = sem("nat_hi_done")
        nat_lo_done = sem("nat_lo_done")
        deg_done = sem("deg_done")
        max_made = sem("max_made")
        ht_ones = sem("ht_ones")
        sum4 = sem("sum4")
        dv = sem("dv")
        stats_done = sem("stats_done")
        rstd_done = sem("rstd_done")
        w3_signed = sem("w3_signed")
        w3_t_ps = sem("w3_t_ps")
        w3_t_done = sem("w3_t_done")
        w0_hi_done = sem("w0_hi_done")
        w0_lo_done = sem("w0_lo_done")
        relu0 = sem("relu0")
        h0_hi_done = sem("h0_hi_done")
        h0_lo_done = sem("h0_lo_done")
        h0_t_ps = sem("h0_t_ps")
        h0_t_done = sem("h0_t_done")
        hw_ps = sem("hw_ps")
        hw_done = sem("hw_done")
        deg_copied = sem("deg_copied")
        dinv_done = sem("dinv_done")
        dinv_scaled = sem("dinv_scaled")
        g_hi_done = sem("g_hi_done")
        g_lo_done = sem("g_lo_done")
        y_ps = sem("y_ps")
        y_taken = sem("y_taken")
        dl = sem("dl")
        ve1 = sem("ve1")
        rs1 = sem("rs1")
        relu1 = sem("relu1")
        h1_hi_done = sem("h1_hi_done")
        h1_lo_done = sem("h1_lo_done")
        ones_col = sem("ones_col")
        amax_part = sem("amax_part")
        amax_all = sem("amax_all")
        amax_neg = sem("amax_neg")
        t_ps = sem("t_ps")
        at_hi_done = sem("at_hi_done")
        e_done = sem("e_done")
        at_lo_done = sem("at_lo_done")
        mask_done = sem("mask_done")
        at_sent = [sem(f"at_sent{b}") for b in range(2)]
        e_sent = [sem(f"e_sent{b}") for b in range(2)]
        l1_ps = sem("l1_ps")
        l1_taken = sem("l1_taken")
        dm = sem("dm")
        n_done = sem("n_done")
        c_done = sem("c_done")
        ve2 = sem("ve2")
        rs2 = sem("rs2")
        relu2 = sem("relu2")
        h2_hi_done = sem("h2_hi_done")
        h2_lo_done = sem("h2_lo_done")
        h2_t_ps = sem("h2_t_ps")
        h2_t_done = sem("h2_t_done")
        wa_done = sem("wa_done")
        w2_hi_done = sem("w2_hi_done")
        w2_lo_done = sem("w2_lo_done")
        sd_ps = sem("sd_ps")
        dmax_part = sem("dmax_part")
        dmax_all = sem("dmax_all")
        d_shift = sem("d_shift")
        up_arg = sem("up_arg")
        exps = sem("exps")
        scaled_w = sem("scaled_w")
        scaled_u = sem("scaled_u")
        ut_ps = sem("ut_ps")
        ut_done = sem("ut_done")
        u_out = sem("u_out")
        u_in = [sem(f"u_in{h}") for h in range(HEADS)]
        ht_ps = sem("ht_ps")
        ht_hi_done = sem("ht_hi_done")
        ht_lo_done = sem("ht_lo_done")
        e_loaded = [sem(f"e_loaded{k}") for k in range(NB // TG)]
        p_done = sem("p_done")
        p_hi_done = sem("p_hi_done")
        p_lo_done = sem("p_lo_done")
        p_used = sem("p_used")
        inv_done = sem("inv_done")
        head_scaled = sem("head_scaled")
        head_added = sem("head_added")
        ba_chain = sem("ba_chain")
        ba_done = sem("ba_done")
        at3_in = [sem(f"at3_in{k}") for k in range(4)]
        ba_t_ps = sem("ba_t_ps")
        ba_t_done = sem("ba_t_done")
        xw_ps = sem("xw_ps")
        xw_done = sem("xw_done")
        o_ps = sem("o_ps")
        o_done = sem("o_done")
        out_sent = sem("out_sent")

        block = ctx.enter_context(nc.Block())

        @block.sync
        def _(sp):
            sp.dma_start(x[:, :, :], x_rows).then_inc(x_in, 16)
            sp.dma_start(w0_f, w0_d.rearrange("(c p) d -> p c d", p=P)).then_inc(w0_in, 16)
            sp.dma_start(w3_f, w3_d.rearrange("(c p) d -> p c d", p=P)).then_inc(w0_in, 16)
            sp.dma_start(bias, b0_d.partition_broadcast(P)).then_inc(w0_in, 16)

            def load_pass1(i, first):
                for b in range(2):
                    for s in range(2):
                        k = 2 * b + s
                        if not first:
                            sp.wait_ge(nat_lo_done, 4 * i + k - 3)
                        sp.dma_start(stage[:, k, :], adj_rows[2 * i + b][:, s * HALF:(s + 1) * HALF]
                                     ).then_inc(half_in[k], 16)

            load_pass1(0, True)
            with nc.sync.Fori(1, NB // 2) as i:
                load_pass1(i, False)

            def load_pass2(i, b, first):
                for s in range(2):
                    k = 2 * b + s
                    if first:
                        sp.wait_ge(nat_lo_done, 4 * (NB // 2 - 1) + k + 1)
                    else:
                        sp.wait_ge(t_ps, 2 * (4 * (i - 1) + k) + 2)
                    sp.dma_start(stage[:, k, :], adj_rows[2 * i + b][:, s * HALF:(s + 1) * HALF]
                                 ).then_inc(half_in[k], 16)

            def store_block(i, b):
                sp.wait_ge(at_lo_done, 4 * (2 * i + b) + 4)
                sp.dma_start(at_dram[2 * i + b], at[:, b, :, :, :].rearrange("p h j n -> p (h j n)")
                             ).then_inc(at_sent[b], 16)
                sp.wait_ge(e_done, 4 * (2 * i + b) + 4)
                sp.dma_start(e_dram[2 * i + b].rearrange("j p n -> p j n"), e_out[:, b, :, :]
                             ).then_inc(e_sent[b], 16)

            for b in range(2):
                load_pass2(0, b, True)
            sp.wait_ge(y_ps, 10)
            sp.wait_ge(amax_part, 1)
            sp.dma_start(w2_f, w2_d.rearrange("(c p) m -> p c m", p=P)).then_inc(w2_in, 16)
            sp.dma_start(a_bc, a2_d.rearrange("h e o -> (h e o)").partition_broadcast(P)
                         ).then_inc(w2_in, 16)
            with nc.sync.Fori(1, NB // 2) as i:
                for b in range(2):
                    load_pass2(i, b, False)
                    store_block(i - 1, b)
            for b in range(2):
                store_block(NB // 2 - 1, b)

            sp.wait_ge(ut_done, 1)
            sp.dma_start(u_dram.rearrange("t h n -> (t h) n"), up_t[0:HEADS * NB, :]).then_inc(u_out, 16)
            sp.wait_ge(u_out, 16)
            for h in range(HEADS):
                sp.dma_start(u_bc[:, h, :].rearrange("p (t n) -> p t n", t=NB),
                             u_dram[:, h, :].partition_broadcast(P)).then_inc(u_in[h], 16)

            e_q = e_dram.rearrange("(q r) (g j) p n -> q g j p r n", r=QB, j=TG)

            def load_e(q, first):
                for g in range(NB // TG):
                    if not first:
                        sp.wait_ge(p_done, (q - 1) * HEADS * NB + (HEADS - 1) * NB + TG * (g + 1))
                    for j in range(TG):
                        sp.dma_start(e_in[:, TG * g + j, :].rearrange("p (r n) -> p r n", r=QB),
                                     e_q[q, g, j]).then_inc(e_loaded[g], 16)

            for b in range(2):
                sp.wait_ge(e_sent[b], 16 * NB // 2)
                sp.wait_ge(at_sent[b], 16 * NB // 2)
            sp.wait_ge(l1_ps, NB)
            sp.wait_ge(h2_lo_done, NB)
            load_e(0, True)
            with nc.sync.Fori(1, NQ) as q:
                load_e(q, False)

            sp.wait_ge(ht_ps, 2 * NB)
            for k in range(4):
                if k == 3:
                    sp.wait_ge(xw_done, 2 * (NQ - 1))
                sp.dma_start(at3[:, k, :, :, :].rearrange("p h j n -> p (h j n)"), at_dram[k]
                             ).then_inc(at3_in[k], 16)

            def store_out(i, k):
                sp.wait_ge(o_done, 4 * i + k + 1)
                sp.dma_start(out_rows[4 * i + k], x[:, 4 * i + k, :]).then_inc(out_sent, 16)

            with nc.sync.Fori(1, NB // 4) as i:
                for k in range(4):
                    sp.wait_ge(o_ps, 4 * i + k - 3)
                    sp.dma_start(at3[:, k, :, :, :].rearrange("p h j n -> p (h j n)"), at_dram[4 * i + k]
                                 ).then_inc(at3_in[k], 16)
                    store_out(i - 1, k)
            for k in range(4):
                store_out(NB // 4 - 1, k)
            sp.wait_ge(out_sent, 16 * NB)

        @block.gpsimd
        def _(pool):
            nc.gpsimd.memset(ident[:, :], 0.0).then_inc(ident_zero, 1)
            nc.gpsimd.memset(ones16[:, :], 1.0).then_inc(consts, 1)
            nc.gpsimd.memset(neg_half[:, :], -0.5).then_inc(consts, 1)
            pool.wait_ge(ident_zero, 1)
            nc.gpsimd.affine_select(out=ident[:, :], in_=ident[:, :], compare_op=ALU.not_equal, fill=1.0,
                                    base=0, pattern=[[-1, P]], channel_multiplier=1).then_inc(ident_zero, 1)
            pool.wait_ge(ident_zero, 2)
            nc.gpsimd.tensor_copy(ident16[:, :], ident[:, :]).then_inc(consts, 1)
            pool.wait_ge(consts, 3)

            pool.wait_ge(stats_done, 1)
            nc.gpsimd.tensor_tensor(rstd[:, :], var_eps[:, :], neg_half[:, :], ALU.pow).then_inc(rstd_done, 1)
            pool.wait_ge(deg_copied, 1)
            nc.gpsimd.tensor_tensor(dinv[:, :], deg[:, :], neg_half[:, :], ALU.pow).then_inc(dinv_done, 1)

            for half in range(2):
                with nc.gpsimd.Fori(half * HBK, (half + 1) * HBK) as i:
                    pool.wait_ge(ve1, i + 1)
                    nc.gpsimd.tensor_tensor(rstd[:, bass.ds(i, 1)], var_eps[:, bass.ds(i, 1)],
                                            neg_half[:, 0:1], ALU.pow).then_inc(rs1, 1)
                if half == 0:
                    pool.wait_ge(amax_part, 1)
                    nc.gpsimd.partition_all_reduce(amax[:, 1:2], amax[:, 0:1], P, RMAX).then_inc(amax_all, 1)
            with nc.gpsimd.Fori(0, NB // 2) as i:
                for b in range(2):
                    pool.wait_ge(n_done, 2 * i + b + 1)
                    nc.gpsimd.tensor_tensor(row_n[:, b, 1:2], row_n[:, b, 0:1], neg_half[:, 0:1],
                                            ALU.pow).then_inc(c_done, 1)
                    pool.wait_ge(ve2, 2 * i + b + 1)
                    nc.gpsimd.tensor_tensor(row_n[:, b, 7:8], row_n[:, b, 6:7], neg_half[:, 0:1],
                                            ALU.pow).then_inc(rs2, 1)

            pool.wait_ge(dmax_part, 1)
            nc.gpsimd.partition_all_reduce(dmax[:, 1, :], dmax[:, 0, :], P, RMAX).then_inc(dmax_all, 1)

            with nc.gpsimd.Fori(0, NQ) as q:
                with nc.gpsimd.Fori(0, HEADS) as h:
                    for r in range(QB):
                        pool.wait_ge(head_scaled, q * (HEADS * QB) + h * QB + r + 1)
                        nc.gpsimd.tensor_tensor(x[:, QB * q + r, :], x[:, QB * q + r, :],
                                                head_out[:, r % 2, :], ALU.add).then_inc(head_added, 1)

        @block.tensor
        def _(pe):
            mm = nc.tensor.matmul
            pe.wait_ge(consts, 3)

            pe.wait_ge(w3_signed, 1)
            for c in range(DC):
                for oc in range(DC):
                    ins = nc.tensor.transpose(ps16(0)[:, (c * DC + oc) * P:(c * DC + oc + 1) * P],
                                              w3_s[:, oc, c * P:(c + 1) * P], ident16[:, :])
            ins.then_inc(w3_t_ps, 1)

            def degrees(j, first, last):
                pe.wait_ge(nat_lo_done, 2 * j + 2)
                for q in range(4):
                    for part in range(2):
                        ins = mm(ps[:, 4 + q, :].rearrange("p (a n) -> p a n", a=4), ones16[:, :],
                                 nat[:, 4 * q:4 * q + 4, part, j, :],
                                 start=(first and part == 0), stop=(last and part == 1))
                return ins

            def h0_transposes(t, b):
                pe.wait_ge(h0_lo_done, t + 1)
                pe.wait_ge(h0_hi_done, t + 1)
                for part, src in enumerate((hn_hi, hn_lo)):
                    for c in range(DC):
                        ins = nc.tensor.transpose(ps16(b)[:, (part * DC + c) * P:(part * DC + c + 1) * P],
                                                  src[:, b, c * P:(c + 1) * P], ident16[:, :])
                ins.then_inc(h0_t_ps, 1)

            def h0_products(t, b, first):
                pe.wait_ge(h0_t_done, t + 1)
                if not first:
                    pe.wait_ge(hw_done, t - 1)
                n = 0
                for ha, wb in ((0, w0_hi), (0, w0_lo), (1, w0_hi)):
                    for c in range(DC):
                        ins = mm(ps[:, 2 + b, 0:D], h0_t[:, b, ha * DC + c, :], wb[:, c, :],
                                 start=(n == 0), stop=(n == 5))
                        n += 1
                ins.then_inc(hw_ps, 1)

            pe.wait_ge(w3_t_done, 1)
            pe.wait_ge(w0_lo_done, 1)

            def load_step(i, first, last):
                for b in range(2):
                    t = 2 * i + b
                    if not (last and b == 1):
                        h0_transposes(t + 1, 1 - b)
                    h0_products(t, b, first)
                    if not (first and b == 0):
                        degrees(t - 1, first and b == 1, False)

            h0_transposes(0, 0)
            load_step(0, True, False)
            with nc.tensor.Fori(1, NB // 2 - 1) as i:
                load_step(i, False, False)
            load_step(NB // 2 - 1, False, True)
            degrees(NB - 1, False, True).then_inc(deg_done, 1)

            def layer0(i, first, only=(0, 1)):
                for b in only:
                    ib = 2 * i + b
                    if not first:
                        pe.wait_ge(y_taken, 2 * i + b - 1)
                    for j in range(NB):
                        if first and b == 0:
                            pe.wait_ge(g_lo_done, j + 1)
                        mm(ps[:, 2 + b, 0:D], nat[:, ib, 0, j, :], g_hi[:, j, :], start=(j == 0), stop=False)
                        mm(ps[:, 2 + b, 0:D], nat[:, ib, 0, j, :], g_lo[:, j, :], start=False, stop=False)
                        ins = mm(ps[:, 2 + b, 0:D], nat[:, ib, 1, j, :], g_hi[:, j, :], start=False,
                                 stop=(j == NB - 1))
                    ins.then_inc(y_ps, 1)

            layer0(0, True)
            with nc.tensor.Fori(1, NB // 2 - 1) as i:
                layer0(i, False)

            def transpose_group(i, b, g, first):
                if g % 2 == 0:
                    k = 2 * b + g // 2
                    pe.wait_ge(half_in[k], 16 * (NB // 2) + 16 * (i + 1))
                if not (first and g < 2):
                    n = 4 * (2 * i + b) + g
                    pe.wait_ge(mask_done, n - 1)
                    pe.wait_ge(e_done, n - 1)
                for a in range(TG):
                    jb = TG * g + a
                    ins = nc.tensor.transpose(ps[:, 4 + g % 2, a * P:(a + 1) * P],
                                              stage[:, 2 * b + g // 2, (jb % HBK) * P:(jb % HBK + 1) * P],
                                              ident[:, :])
                ins.then_inc(t_ps, 1)

            def products1(i, b, g, first):
                ib = 2 * i + b
                pe.wait_ge(mask_done, 4 * ib + g + 1)
                if g == 0 and not first:
                    pe.wait_ge(l1_taken, ib - 1)
                for a in range(TG):
                    j = TG * g + a
                    if first and b == 0:
                        pe.wait_ge(h1_lo_done, j + 1)
                        if j == 0:
                            pe.wait_ge(ones_col, 1)
                    if first and b == 1 and j == 0:
                        pe.wait_ge(y_taken, NB)
                    s, e = (j == 0), (j == NB - 1)
                    mm(ps[:, 2 * b, 0:DE], at[:, b, 0, j, :], h1_hi[:, j, 0:DE], start=s, stop=False)
                    mm(ps[:, 2 * b, 0:D], at[:, b, 0, j, :], h1_lo[:, j, :], start=False, stop=False)
                    mm(ps[:, 2 * b, 0:DE], at[:, b, 1, j, :], h1_hi[:, j, 0:DE], start=False, stop=e)
                    mm(ps[:, 2 * b + 1, 0:D], mask[:, b, j, :], h1_lo[:, j, :], start=s, stop=False,
                       skip_group_check=True)
                    ins = mm(ps[:, 2 * b + 1, 0:DE], mask[:, b, j, :], h1_hi[:, j, 0:DE], start=False, stop=e,
                             skip_group_check=True)
                return ins

            def h2_transposes(t, b):
                pe.wait_ge(h2_hi_done, t + 1)
                pe.wait_ge(h2_lo_done, t + 1)
                for part, src in enumerate((h2_hi, h2_lo)):
                    for c in range(DC):
                        ins = nc.tensor.transpose(ps16(6)[:, (part * DC + c) * P:(part * DC + c + 1) * P],
                                                  src[:, b, c * P:(c + 1) * P], ident16[:, :])
                ins.then_inc(h2_t_ps, 1)

            def scores(t):
                pe.wait_ge(h2_t_done, t + 1)
                n = 0
                for ha, wb in ((0, wa_hi), (0, wa_lo), (1, wa_hi)):
                    for c in range(DC):
                        ins = mm(ps[:, 7, bass.ds(t * (2 * HEADS), 2 * HEADS)],
                                 h2_t[:, ha * DC + c, bass.ds(t * P, P)], wb[:, c, :], start=(n == 0),
                                 stop=(n == 5), skip_group_check=True)
                        n += 1
                ins.then_inc(sd_ps, 1)

            def layer1(i, first, last):
                for b in range(2):
                    for g in range(NB // TG):
                        if b == 0:
                            transpose_group(i, 1, g, False)
                        elif not last:
                            transpose_group(i + 1, 0, g, False)
                        ins = products1(i, b, g, first)
                        if g == NB // TG - 1:
                            ins.then_inc(l1_ps, 1)
                        if g == 1 and not first:
                            scores(2 * i + b - 2)
                        if g == 3 and not (first and b == 0):
                            h2_transposes(2 * i + b - 1, 1 - b)

            pe.wait_ge(deg_copied, 1)
            for b in range(2):
                for g in (2 * b, 2 * b + 1):
                    transpose_group(0, 0, g, True)
                layer0(NB // 2 - 1, False, (b,))
            layer1(0, True, False)
            pe.wait_ge(wa_done, 1)
            with nc.tensor.Fori(1, NB // 2 - 1) as i:
                layer1(i, False, False)
            layer1(NB // 2 - 1, False, True)
            def ht_block(i, first):
                for b in range(2):
                    t = 2 * i + b
                    if first and b == 0:
                        pe.wait_ge(w2_lo_done, 1)
                    for half in range(2):
                        if not first:
                            pe.wait_ge(ht_lo_done, HEADS * (t - 2) + 2 * half + 2)
                        n = 0
                        for ha, wb in ((0, w2_hi), (0, w2_lo), (1, w2_hi)):
                            for c in range(DC):
                                ins = mm(ps[:, 2 * b + half, :], h2_t[:, ha * DC + c, bass.ds(t * P, P)],
                                         wb[:, c, 512 * half:512 * half + 512], start=(n == 0), stop=(n == 5))
                                n += 1
                        ins.then_inc(ht_ps, 1)

            scores(NB - 2)
            pe.wait_ge(l1_taken, NB)
            ht_block(0, True)
            h2_transposes(NB - 1, 1)
            scores(NB - 1)
            pe.wait_ge(scaled_u, 1)
            nc.tensor.transpose(ps[0:HEADS * NB, 4, 0:P], up_i[:, :, :].rearrange("p t h -> p (t h)"),
                                ident[:, :]).then_inc(ut_ps, 1)
            with nc.tensor.Fori(1, NB // 2) as i:
                ht_block(i, False)

            def head_products(q, head, first):
                b = head % 2
                group = q * HEADS + head
                for j in range(NB):
                    step = group * NB + j
                    if first and head == 0 and j == 0:
                        pe.wait_ge(ht_lo_done, HEADS * NB)
                        pe.wait_ge(ht_hi_done, HEADS * NB)
                        pe.wait_ge(ht_ones, 1)
                    if not first and head == 2 and j == 0:
                        pe.wait_ge(xw_done, 2 * q)
                    pe.wait_ge(p_hi_done, step + 1)
                    pe.wait_ge(p_lo_done, step + 1)
                    s, e = (j == 0), (j == NB - 1)
                    slot = j % 4
                    for r in range(QB):
                        if j == 0 and not (first and head < 2):
                            pe.wait_ge(head_scaled, (group - 2) * QB + r + 1)
                        bank = 4 * b + r
                        hi = p_hi[:, slot, r * P:(r + 1) * P]
                        lo = p_lo[:, slot, r * P:(r + 1) * P]
                        mm(ps[:, bank, 0:DE], hi, ht_hi[:, head, j, 0:DE], start=s, stop=False)
                        mm(ps[:, bank, 0:DE], hi, ht_lo[:, head, j, 0:DE], start=False, stop=False)
                        ins = mm(ps[:, bank, 0:DE], lo, ht_hi[:, head, j, 0:DE], start=False, stop=e)
                    ins.then_inc(p_used, 1)
                    if not first and head == 1:
                        if j == 5:
                            pe.wait_ge(head_scaled, group * QB)
                        if j in (5, 6):
                            binary_turn(q - 1, j - 5, j - 5, ba_loop)
                        if j in (10, 11):
                            binary_product(q - 1, j - 10, 2 + j - 10, bat_loop)

            def binary_turn(q, pair, bank, ba):
                pe.wait_ge(ba_done, QB * q + 2 * pair + 2)
                for k in range(2 * DC):
                    ins = nc.tensor.transpose(ps16(bank)[:, k * P:(k + 1) * P],
                                              ba[:, 2 * pair + k // DC, (k % DC) * P:(k % DC + 1) * P],
                                              ident16[:, :])
                ins.then_inc(ba_t_ps, 1)

            def binary_product(q, pair, bank, bat):
                pe.wait_ge(ba_t_done, 2 * q + pair + 1)
                for k in range(2 * DC):
                    ins = mm(ps[:, bank, (k // DC) * D:(k // DC + 1) * D], bat[:, pair, k, :],
                             bw_t[:, k % DC, :], start=(k % DC == 0), stop=(k % DC == DC - 1))
                ins.then_inc(xw_ps, 1)

            def quarter(q, first):
                for head in range(HEADS):
                    head_products(q, head, first)

            quarter(0, True)
            with nc.tensor.Fori(1, NQ) as q:
                quarter(q, False)

            def layer3_products(k, blocks):
                for j in blocks:
                    mm(ps[:, k, 0:D], at3[:, k, 0, j, :], xw[:, j, :], start=(j == 0), stop=False)
                    ins = mm(ps[:, k, 0:D], at3[:, k, 1, j, :], xw[:, j, :], start=False, stop=(j == NB - 1))
                return ins

            pe.wait_ge(xw_done, 2 * (NQ - 1))
            pe.wait_ge(head_scaled, (NQ * HEADS - 1) * QB)
            for k in range(4):
                pe.wait_ge(at3_in[k], 16)
                layer3_products(k, range(NB - QB))
            pe.wait_ge(head_scaled, NQ * HEADS * QB)
            for pair in range(2):
                binary_turn(NQ - 1, pair, 4 + pair, ba_tail)
            for pair in range(2):
                binary_product(NQ - 1, pair, 6 + pair, bat_tail)
            pe.wait_ge(xw_done, 2 * NQ)
            for k in range(4):
                layer3_products(k, range(NB - QB, NB)).then_inc(o_ps, 1)
            with nc.tensor.Fori(1, NB // 4) as i:
                for k in range(4):
                    pe.wait_ge(at3_in[k], 16 * (i + 1))
                    pe.wait_ge(o_done, 4 * (i - 1) + k + 1)
                    layer3_products(k, range(NB)).then_inc(o_ps, 1)

        @block.scalar
        def _(act):
            copy = ACT.Copy

            act.wait_ge(w0_in, 48)
            nc.scalar.activation(w0_hi, w0_f, copy, scale=W_SCALE).then_inc(w0_hi_done, 1)
            act.wait_ge(w3_t_ps, 1)
            nc.scalar.activation(bw_t[:, :, :].rearrange("p c d -> p (c d)"), ps16(0)[:, 0:DC * D], copy
                                 ).then_inc(w3_t_done, 1)

            def adj_high(j, s, k, need):
                act.wait_ge(half_in[k], need)
                nc.scalar.activation(nat[:, s * HBK:(s + 1) * HBK, 0, j, :],
                                     stage[:, k, :].rearrange("p (a n) -> p a n", a=HBK), copy,
                                     scale=ADJ_SCALE).then_inc(nat_hi_done, 1)

            def h0_turned(t, b, first):
                act.wait_ge(h0_t_ps, t + 1)
                if not first:
                    act.wait_ge(hw_ps, t - 1)
                nc.scalar.activation(h0_t[:, b, :, :].rearrange("p a n -> p (a n)"),
                                     ps16(b)[:, 0:2 * DC * P], copy).then_inc(h0_t_done, 1)

            def hw_copy(t, b):
                act.wait_ge(hw_ps, t + 1)
                nc.scalar.activation(hw[:, t, :], ps[:, 2 + b, 0:D], copy,
                                     scale=1.0 / (H_SCALE * W_SCALE)).then_inc(hw_done, 1)

            def load_step(i, first, last):
                for b in range(2):
                    t = 2 * i + b
                    adj_high(t, 0, 2 * b, 16 * (i + 1))
                    adj_high(t, 1, 2 * b + 1, 16 * (i + 1))
                    if not (last and b == 1):
                        h0_turned(t + 1, 1 - b, first and b == 0)
                    if not (first and b == 0):
                        hw_copy(t - 1, 1 - b)

            h0_turned(0, 0, True)
            load_step(0, True, False)
            with nc.scalar.Fori(1, NB // 2 - 1) as i:
                load_step(i, False, False)
            load_step(NB // 2 - 1, False, True)
            hw_copy(NB - 1, 1)

            act.wait_ge(dinv_scaled, 2)
            act.wait_ge(hw_done, NB)
            act.wait_ge(hw_ps, NB)
            for t in range(NB):
                nc.scalar.activation(g_hi[:, t, :], hw[:, t, :], copy,
                                     scale=dinv_in[:, t:t + 1]).then_inc(g_hi_done, 1)

            def h1_high(i, b):
                act.wait_ge(relu1, 2 * i + b + 1)
                act.wait_ge(rs1, 2 * i + b + 1)
                nc.scalar.activation(h1_hi[:, 2 * i + b, 0:D], ln_relu[:, b, :], copy,
                                     scale=rstd[:, bass.ds(2 * i + b, 1)]).then_inc(h1_hi_done, 1)

            with nc.scalar.Fori(0, NB // 2 - 1) as i:
                for b in range(2):
                    h1_high(i, b)

            def adj_t_group(i, b, g, first):
                n = 4 * (2 * i + b) + g
                act.wait_ge(t_ps, n + 1)
                if g == 0 and not first:
                    act.wait_ge(l1_ps, 2 * i + b - 1)
                    act.wait_ge(at_sent[b], 16 * i)
                    act.wait_ge(e_sent[b], 16 * i)
                nc.scalar.activation(at[:, b, 0, TG * g:TG * g + TG, :].rearrange("p j n -> p (j n)"),
                                     ps[:, 4 + g % 2, :], copy, scale=ADJ_SCALE).then_inc(at_hi_done, 1)
                nc.scalar.activation(e_out[:, b, TG * g:TG * g + TG, :].rearrange("p j n -> p (j n)"),
                                     ps[:, 4 + g % 2, :], ACT.Exp, bias=amax[:, 2:3]).then_inc(e_done, 1)

            def h2_high(t, b):
                act.wait_ge(relu2, t + 1)
                act.wait_ge(rs2, t + 1)
                nc.scalar.activation(h2_hi[:, b, :], ln_relu[:, b, :], copy,
                                     scale=row_n[:, b, 7:8]).then_inc(h2_hi_done, 1)

            def h2_turned(t):
                act.wait_ge(h2_t_ps, t + 1)
                nc.scalar.activation(h2_t[:, :, bass.ds(t * P, P)],
                                     ps16(6)[:, 0:2 * DC * P].rearrange("p (a n) -> p a n", a=2 * DC), copy
                                     ).then_inc(h2_t_done, 1)

            act.wait_ge(amax_neg, 1)
            act.wait_ge(y_ps, NB - 3)
            for b in range(2):
                for g in (2 * b, 2 * b + 1):
                    adj_t_group(0, 0, g, True)
                h1_high(NB // 2 - 1, b)
            for g in range(NB // TG):
                adj_t_group(0, 1, g, True)
            act.wait_ge(w2_in, 32)
            act.wait_ge(y_ps, NB)
            nc.scalar.activation(w2_hi, w2_f, copy, scale=W_SCALE).then_inc(w2_hi_done, 1)

            def layer1(i):
                for b in range(2):
                    for g in range(NB // TG):
                        adj_t_group(i, b, g, False)
                        if g == 2:
                            h2_high(2 * i + b - 2, b)
                    h2_turned(2 * i + b - 2)

            with nc.scalar.Fori(1, NB // 2) as i:
                layer1(i)
            for b in range(2):
                h2_high(NB - 2 + b, b)
                h2_turned(NB - 2 + b)

            act.wait_ge(d_shift, 1)
            flat = "p t h -> p (t h)"
            nc.scalar.activation(vp_j[:, :, :].rearrange(flat), w_j[:, :, :].rearrange(flat), ACT.Exp,
                                 scale=SLOPE).then_inc(exps, 1)
            act.wait_ge(exps, 1)
            nc.scalar.activation(w_j[:, :, :].rearrange(flat), w_j[:, :, :].rearrange(flat), ACT.Exp,
                                 scale=1.0 - SLOPE).then_inc(exps, 1)
            act.wait_ge(up_arg, 1)
            nc.scalar.activation(up_i[:, :, :].rearrange(flat), up_i[:, :, :].rearrange(flat), ACT.Exp,
                                 scale=-(1.0 - SLOPE)).then_inc(exps, 1)

            def ht_high(i):
                for b in range(2):
                    t = 2 * i + b
                    for h in range(HEADS):
                        act.wait_ge(ht_ps, 2 * t + h // 2 + 1)
                        nc.scalar.activation(ht_hi[:, h, t, 0:D],
                                             ps[:, 2 * b + h // 2, (h % 2) * D:(h % 2 + 1) * D], copy,
                                             scale=vp_j[:, t, h:h + 1]).then_inc(ht_hi_done, 1)

            act.wait_ge(exps, 3)
            for b in range(2):
                act.wait_ge(at_sent[b], 16 * NB // 2)
                act.wait_ge(e_sent[b], 16 * NB // 2)
            ht_high(0)
            act.wait_ge(ut_ps, 1)
            nc.scalar.activation(up_t[0:HEADS * NB, :], ps[0:HEADS * NB, 4, 0:P], copy).then_inc(ut_done, 1)
            with nc.scalar.Fori(1, NB // 2 - 2) as i:
                ht_high(i)
            for pair in range(2):
                for j in (2 * pair, 2 * pair + 1):
                    act.wait_ge(p_done, j + 1)
                    nc.scalar.activation(p_hi[:, j, :], prob[:, j, :], copy).then_inc(p_hi_done, 1)
                ht_high(NB // 2 - 2 + pair)

            def scale_head(group, b, r, early):
                if r == 0:
                    act.wait_ge(inv_done, group + 1)
                if not (early and r < 2):
                    act.wait_ge(head_added, group * QB + r - 1)
                nc.scalar.activation(head_out[:, r % 2, :], ps[:, 4 * b + r, 0:D], copy,
                                     scale=inv_l[:, b, r:r + 1]).then_inc(head_scaled, 1)

            def hold(r, k):
                nc.scalar.activation(held_act[:, 2 * r + k:2 * r + k + 1], neg_half[:, 0:1], copy)

            def binary_input(part, q, r, ba):
                t = QB * q + r
                n = 3 * t
                if part == 1:
                    act.wait_ge(head_added, (q + 1) * (HEADS * QB) - QB + r + 1)
                    nc.scalar.activation(ba[:, r, :], x[:, t, :], copy, scale=-1.0 / D,
                                         accum_out=neg_mean[:, r:r + 1]).then_inc(ba_chain, 1)
                elif part == 2:
                    act.wait_ge(ba_chain, 2 * t + 1)
                    hold(r, 0)
                    nc.scalar.activation(ba[:, r, :], x[:, t, :], ACT.Sign, bias=neg_mean[:, r:r + 1]
                                         ).then_inc(ba_chain, 1)
                else:
                    act.wait_ge(ba_chain, 2 * t + 2)
                    hold(r, 1)
                    nc.scalar.activation(ba[:, r, :], ba[:, r, :], ACT.Relu).then_inc(ba_done, 1)

            def binary_turned(q, pair, bat, bank=0):
                act.wait_ge(ba_t_ps, 2 * q + pair + 1)
                nc.scalar.activation(bat[:, pair, :, :].rearrange("p k n -> p (k n)"),
                                     ps16(bank + pair)[:, 0:2 * DC * P], copy).then_inc(ba_t_done, 1)

            def binary_out(q, pair, bank=2):
                act.wait_ge(xw_ps, 2 * q + pair + 1)
                nc.scalar.activation(xw[:, bass.ds(QB * q + 2 * pair, 2), :].rearrange("p t d -> p (t d)"),
                                     ps[:, bank + pair, :], copy, scale=1.0 / ADJ_SCALE).then_inc(xw_done, 1)

            def head_high(q, hp, b, first, second, norms=False, turns=False):
                head = 2 * hp + b
                group = q * HEADS + head
                for j in range(EARLY if first else 0, NB):
                    step = group * NB + j
                    act.wait_ge(p_done, step + 1)
                    if not (first and j < 4):
                        act.wait_ge(p_used, step - 3)
                    nc.scalar.activation(p_hi[:, j % 4, :], prob[:, j % 4, :], copy).then_inc(p_hi_done, 1)
                    if not first and 4 <= j < 4 + QB:
                        scale_head(group - 1, 1 - b, j - 4, second)
                    if norms and j >= 8:
                        for part in ((1,) if j % 2 == 0 else (2, 3)):
                            binary_input(part, q - 1, (j - 8) // 2, ba_loop)
                    if turns and j in (10, 11):
                        binary_turned(q - 1, j - 10, bat_loop)
                    if turns and j == 15:
                        for pair in range(2):
                            binary_out(q - 1, pair)

            head_high(0, 0, 0, True, False)
            head_high(0, 0, 1, False, True)
            for b in range(2):
                head_high(0, 1, b, False, False)
            with nc.scalar.Fori(1, NQ) as q:
                for hp in range(HEADS // 2):
                    for b in range(2):
                        head_high(q, hp, b, False, False, norms=(hp == 0 and b == 0),
                                  turns=(hp == 0 and b == 1))
            for r in range(QB):
                scale_head(NQ * HEADS - 1, 1, r, False)
            for r in range(QB):
                for part in (1, 2, 3):
                    binary_input(part, NQ - 1, r, ba_tail)
            for pair in range(2):
                binary_turned(NQ - 1, pair, bat_tail, 4)
            for pair in range(2):
                binary_out(NQ - 1, pair, 6)

        @block.vector
        def _(dve):
            v = nc.vector
            made = [0]

            def hold(k):
                v.memset(held[:, k:k + 1], 0.0)

            def link(ins):
                made[0] += 1
                ins.then_inc(dv, 1)
                dve.wait_ge(dv, made[0])

            dve.wait_ge(w0_in, 48)
            v.tensor_scalar(w3_s, w3_f, 0.0, None, ALU.is_lt).then_inc(dv, 1)
            made[0] += 1
            dve.wait_ge(dv, made[0])
            v.scalar_tensor_tensor(w3_s, w3_f, 0.0, w3_s, ALU.is_gt, ALU.subtract).then_inc(w3_signed, 1)
            dve.wait_ge(w0_hi_done, 1)
            v.scalar_tensor_tensor(w0_lo, w0_f, W_SCALE, w0_hi, ALU.mult, ALU.subtract).then_inc(w0_lo_done, 1)

            dve.wait_ge(x_in, 16)
            for t in range(NB):
                ins = v.bn_stats(stats[:, t, :], x[:, t, :])
            link(ins)
            for t in range(NB):
                ins = v.bn_aggr(mean_var[:, t, :], stats[:, t, :])
            link(ins)
            v.tensor_scalar(var_eps[:, :], mean_var[:, :, 1], LN_EPS, H_SCALE ** -2, ALU.add, ALU.mult
                            ).then_inc(stats_done, 1)

            def adj_low(j, s, k, n):
                dve.wait_ge(nat_hi_done, n + 1)
                v.scalar_tensor_tensor(nat[:, s * HBK:(s + 1) * HBK, 1, j, :],
                                       stage[:, k, :].rearrange("p (a n) -> p a n", a=HBK), ADJ_SCALE,
                                       nat[:, s * HBK:(s + 1) * HBK, 0, j, :], ALU.mult, ALU.subtract
                                       ).then_inc(nat_lo_done, 1)

            def relu_shift(t, b):
                v.tensor_scalar(hrelu[:, b, :], x[:, t, :], mean_var[:, t, 0:1], 0.0, ALU.subtract, ALU.max
                                ).then_inc(relu0, 1)

            def h0_parts(t, b, first):
                dve.wait_ge(relu0, t + 1)
                if not first:
                    dve.wait_ge(h0_t_ps, t - 1)
                v.tensor_scalar(hn_hi[:, b, :], hrelu[:, b, :], rstd[:, bass.ds(t, 1)], None, ALU.mult
                                ).then_inc(h0_hi_done, 1)
                dve.wait_ge(h0_hi_done, t + 1)
                v.scalar_tensor_tensor(hn_lo[:, b, :], hrelu[:, b, :], rstd[:, bass.ds(t, 1)], hn_hi[:, b, :],
                                       ALU.mult, ALU.subtract).then_inc(h0_lo_done, 1)

            def load_step(i, left):
                for b in range(2):
                    t = 2 * i + b
                    adj_low(t, 0, 2 * b, 2 * t)
                    adj_low(t, 1, 2 * b + 1, 2 * t + 1)
                    if left >= 2:
                        h0_parts(t + 2, b, False)
                    if left >= 4:
                        dve.wait_ge(h0_lo_done, t + 3)
                        relu_shift(t + 4, b)

            for b in range(2):
                relu_shift(b, b)
            dve.wait_ge(rstd_done, 1)
            for b in range(2):
                h0_parts(b, b, True)
            dve.wait_ge(h0_lo_done, 2)
            for b in range(2):
                relu_shift(2 + b, b)
            with nc.vector.Fori(0, NB // 2 - 2) as i:
                load_step(i, 4)
            load_step(NB // 2 - 2, 2)
            load_step(NB // 2 - 1, 0)

            dve.wait_ge(deg_done, 1)
            for t in range(NB):
                ins = v.tensor_tensor_reduce(junk[:, t % JUNK, :], ps[:, 4 + t // 4, (t % 4) * P:(t % 4 + 1) * P],
                                             ident[:, :], 1.0, 0.0, ALU.mult, ALU.add, deg[:, t:t + 1])
                if t == JUNK - 1:
                    link(ins)
            ins.then_inc(deg_copied, 1)
            dve.wait_ge(dinv_done, 1)
            v.tensor_scalar(dinv_in[:, :], dinv[:, :], 256.0, None, ALU.mult).then_inc(dinv_scaled, 1)
            v.tensor_scalar(dinv_out[:, :], dinv[:, :], 1.0 / 256.0, None, ALU.mult).then_inc(dinv_scaled, 1)
            dve.wait_ge(dinv_scaled, 2)
            dve.wait_ge(hw_done, NB)
            for t in range(NB):
                dve.wait_ge(g_hi_done, t + 1)
                v.scalar_tensor_tensor(g_lo[:, t, :], hw[:, t, :], dinv_in[:, t:t + 1], g_hi[:, t, :],
                                       ALU.mult, ALU.subtract).then_inc(g_lo_done, 1)
            dve.wait_ge(g_lo_done, NB)
            v.memset(h1_hi[:, :, D:DE], 1.0).then_inc(ones_col, 1)
            v.memset(nat_max, 0.0).then_inc(max_made, 1)

            CHAIN0 = 3

            def h1_low(t, b):
                dve.wait_ge(h1_hi_done, t + 1)
                v.scalar_tensor_tensor(h1_lo[:, t, :], ln_relu[:, b, :], rstd[:, bass.ds(t, 1)],
                                       h1_hi[:, t, 0:D], ALU.mult, ALU.subtract).then_inc(h1_lo_done, 1)

            def layer0(t, b, maxima, first=False):
                if maxima:
                    for m in range(2):
                        dve.wait_ge(max_made, 2 * t + m + 1)
                        v.tensor_tensor(nat_max, nat_max,
                                        nat[:, 2 * t + m, 0, :, :].rearrange("p a n -> p (a n)"), ALU.max
                                        ).then_inc(max_made, 1)
                v.tensor_tensor(x[:, t, :], x[:, t, :], bias, ALU.add).then_inc(dl, 1)
                dve.wait_ge(dl, CHAIN0 * t + 1)
                dve.wait_ge(y_ps, t + 1)
                v.scalar_tensor_tensor(x[:, t, :], ps[:, 2 + b, 0:D], dinv_out[:, bass.ds(t, 1)], x[:, t, :],
                                       ALU.mult, ALU.add).then_inc(y_taken, 1)
                if not first:
                    h1_low(t - 1, 1 - b)
                dve.wait_ge(y_taken, t + 1)
                hold(0 + 2 * (b % 2))
                v.bn_stats(stats[:, b, :], x[:, t, :]).then_inc(dl, 1)
                dve.wait_ge(dl, CHAIN0 * t + 2)
                hold(1 + 2 * (b % 2))
                v.bn_aggr(mean_var[:, b, :], stats[:, b, :]).then_inc(dl, 1)
                dve.wait_ge(dl, CHAIN0 * t + 3)
                v.tensor_scalar(var_eps[:, bass.ds(t, 1)], mean_var[:, b, 1:2], LN_EPS, H_SCALE ** -2,
                                ALU.add, ALU.mult).then_inc(ve1, 1)
                v.tensor_scalar(ln_relu[:, b, :], x[:, t, :], mean_var[:, b, 0:1], 0.0, ALU.subtract,
                                ALU.max).then_inc(relu1, 1)

            def w2_a(c):
                for h in range(HEADS):
                    for side in range(2):
                        k = side * HEADS + h
                        link(v.tensor_tensor_reduce(wa_junk, w2_f[:, c, h * D:(h + 1) * D],
                                                    a_bc[:, (2 * h + side) * D:(2 * h + side + 1) * D],
                                                    W_SCALE, 0.0, ALU.mult, ALU.add, wa[:, c, k:k + 1]))

            layer0(0, 0, True, True)
            layer0(1, 1, True)
            with nc.vector.Fori(1, NB // 4) as i:
                for b in range(2):
                    layer0(2 * i + b, b, True)
            dve.wait_ge(max_made, NB + 1)
            v.tensor_reduce(amax[:, 0:1], nat_max, AX_X, ALU.max).then_inc(amax_part, 1)
            with nc.vector.Fori(NB // 4, NB // 2 - 2) as i:
                for b in range(2):
                    layer0(2 * i + b, b, False)
            dve.wait_ge(w2_in, 32)
            for b in range(2):
                layer0(NB - 4 + b, b, False)
                w2_a(b)
            link(v.tensor_copy(wa_hi[:, :, :], wa[:, :, :]))
            v.tensor_tensor(wa_lo[:, :, :], wa[:, :, :], wa_hi[:, :, :], ALU.subtract).then_inc(wa_done, 1)
            dve.wait_ge(amax_all, 1)
            v.tensor_scalar(amax[:, 2:3], amax[:, 1:2], -1.0 / ADJ_SCALE, None, ALU.mult).then_inc(amax_neg, 1)

            def adj_t_group(i, b, g):
                n = 4 * (2 * i + b) + g
                dve.wait_ge(e_done, n + 1)
                v.scalar_tensor_tensor(at[:, b, 1, TG * g:TG * g + TG, :].rearrange("p j n -> p (j n)"),
                                       ps[:, 4 + g % 2, :], ADJ_SCALE,
                                       at[:, b, 0, TG * g:TG * g + TG, :].rearrange("p j n -> p (j n)"),
                                       ALU.mult, ALU.subtract).then_inc(at_lo_done, 1)
                v.tensor_scalar(mask[:, b, TG * g:TG * g + TG, :].rearrange("p j n -> p (j n)"),
                                ps[:, 4 + g % 2, :], 0.0, None, ALU.is_gt).then_inc(mask_done, 1)

            for b in range(2):
                for g in (2 * b, 2 * b + 1):
                    adj_t_group(0, 0, g)
                layer0(NB - 2 + b, b, False)
            h1_low(NB - 1, 1)

            CHAIN1 = 8

            def after(t, k, ins):
                ins.then_inc(dm, 1)
                dve.wait_ge(dm, CHAIN1 * t + k)

            def row_counts(t, b):
                rn = row_n[:, b, :]
                dve.wait_ge(l1_ps, t + 1)
                v.tensor_scalar(rn[:, 0:1], ps[:, 2 * b + 1, D:DE], NORM_EPS ** 2, None, ALU.max
                                ).then_inc(n_done, 1)
                v.tensor_scalar(rn[:, 2:3], ps[:, 2 * b, D:DE], 1.0 / ADJ_SCALE, None, ALU.mult).then_inc(dm, 1)

            def row_sums(t, b):
                rn = row_n[:, b, :]
                dve.wait_ge(dm, CHAIN1 * t + 1)
                dve.wait_ge(c_done, t + 1)
                after(t, 2, v.scalar_tensor_tensor(rn[:, 3:4], ps[:, 2 * b + 1, D:DE], rn[:, 1:2], rn[:, 2:3],
                                                ALU.mult, ALU.add))
                after(t, 3, v.reciprocal(rn[:, 4:5], rn[:, 3:4]))
                v.tensor_scalar(rn[:, 5:6], rn[:, 1:2], rn[:, 4:5], 1.0 / H_SCALE, ALU.mult, ALU.mult
                                ).then_inc(dm, 1)
                after(t, 5, v.tensor_scalar(rn[:, 8:9], rn[:, 4:5], 1.0 / (H_SCALE * ADJ_SCALE), None, ALU.mult))
                after(t, 6, v.scalar_tensor_tensor(x[:, t, :], ps[:, 2 * b, 0:D], rn[:, 8:9], x[:, t, :],
                                                ALU.mult, ALU.add))
                v.scalar_tensor_tensor(x[:, t, :], ps[:, 2 * b + 1, 0:D], rn[:, 5:6], x[:, t, :],
                                       ALU.mult, ALU.add).then_inc(l1_taken, 1)

            def row_norm(t, b):
                rn = row_n[:, b, :]
                dve.wait_ge(l1_taken, t + 1)
                hold(0 + 2 * (b % 2))
                after(t, 7, v.bn_stats(stats[:, b, :], x[:, t, :]))
                hold(1 + 2 * (b % 2))
                after(t, 8, v.bn_aggr(mean_var[:, b, :], stats[:, b, :]))
                v.tensor_scalar(rn[:, 6:7], mean_var[:, b, 1:2], LN_EPS, H_SCALE ** -2, ALU.add, ALU.mult
                                ).then_inc(ve2, 1)
                v.tensor_scalar(ln_relu[:, b, :], x[:, t, :], mean_var[:, b, 0:1], 0.0, ALU.subtract, ALU.max
                                ).then_inc(relu2, 1)

            def h2_low(t, b):
                dve.wait_ge(h2_hi_done, t + 1)
                v.scalar_tensor_tensor(h2_lo[:, b, :], ln_relu[:, b, :], row_n[:, b, 7:8], h2_hi[:, b, :],
                                       ALU.mult, ALU.subtract).then_inc(h2_lo_done, 1)

            def layer1(i, b, low):
                steps = (row_counts, row_sums, row_norm, h2_low)
                for g in range(NB // TG):
                    if low and g < 1:
                        row_counts(2 * i + b - 2, b)
                    adj_t_group(i, b, g)
                    if low and g < 3:
                        steps[g + 1](2 * i + b - 2, b)

            layer1(0, 1, False)
            dve.wait_ge(w2_hi_done, 1)
            v.scalar_tensor_tensor(w2_lo, w2_f, W_SCALE, w2_hi, ALU.mult, ALU.subtract).then_inc(w2_lo_done, 1)
            with nc.vector.Fori(1, NB // 2) as i:
                for b in range(2):
                    layer1(i, b, True)
            for b in range(2):
                row_counts(NB - 2 + b, b)
                row_sums(NB - 2 + b, b)
                row_norm(NB - 2 + b, b)
                h2_low(NB - 2 + b, b)

            dve.wait_ge(sd_ps, NB)
            link(v.tensor_scalar(sd[:, :, :].rearrange("p t k -> p (t k)"), ps[:, 7, 0:2 * HEADS * NB],
                                 1.0 / (H_SCALE * W_SCALE), None, ALU.mult))
            v.tensor_reduce(dmax[:, 0, :], sd[:, :, HEADS:2 * HEADS].rearrange("p t h -> p h t"), AX_X, ALU.max
                            ).then_inc(dmax_part, 1)
            dve.wait_ge(dmax_all, 1)
            dmax_bc = dmax[:, 1:2, :].broadcast_to([P, NB, HEADS])
            v.tensor_tensor(w_j[:, :, :], sd[:, :, HEADS:2 * HEADS], dmax_bc, ALU.subtract).then_inc(d_shift, 1)
            link(v.tensor_tensor(up_i[:, :, :], sd[:, :, 0:HEADS], dmax_bc, ALU.add))
            v.tensor_scalar(up_i[:, :, :], up_i[:, :, :], 0.0, None, ALU.max).then_inc(up_arg, 1)
            dve.wait_ge(exps, 3)
            v.tensor_scalar(up_i[:, :, :], up_i[:, :, :], P_SCALE, None, ALU.mult).then_inc(scaled_u, 1)
            v.tensor_scalar(w_j[:, :, :], w_j[:, :, :], P_SCALE, None, ALU.mult).then_inc(scaled_w, 1)
            for b in range(2):
                dve.wait_ge(at_sent[b], 16 * NB // 2)
                dve.wait_ge(e_sent[b], 16 * NB // 2)
            vp_cols = vp_j[:, :, :].rearrange("p t h -> p h t")
            link(v.tensor_scalar(ht_hi[:, :, :, D], vp_cols, H_SCALE * W_SCALE, None, ALU.mult))
            v.scalar_tensor_tensor(ht_lo[:, :, :, D], vp_cols, H_SCALE * W_SCALE, ht_hi[:, :, :, D],
                                   ALU.mult, ALU.subtract).then_inc(ht_ones, 1)
            def numerators(q, h, j, step):
                if h == 0 and j % TG == 0:
                    dve.wait_ge(e_loaded[j // TG], 16 * TG * (q + 1))
                v.scalar_tensor_tensor(prob[:, j % 4, :], u_bc[:, h, bass.ds(q * (QB * P), QB * P)],
                                       w_j[:, j, h:h + 1], e_in[:, j, :], ALU.max, ALU.mult).then_inc(p_done, 1)

            def low_part(j, step):
                dve.wait_ge(p_hi_done, step + 1)
                v.tensor_tensor(p_lo[:, j % 4, :], prob[:, j % 4, :], p_hi[:, j % 4, :], ALU.subtract
                                ).then_inc(p_lo_done, 1)

            def ht_low(i):
                for b in range(2):
                    for h in range(HEADS):
                        n = HEADS * (2 * i + b) + h
                        if h % 2 == 0:
                            dve.wait_ge(ht_hi_done, n + 2)
                        v.scalar_tensor_tensor(ht_lo[:, h, 2 * i + b, 0:D],
                                               ps[:, 2 * b + h // 2, (h % 2) * D:(h % 2 + 1) * D],
                                               vp_j[:, 2 * i + b, h:h + 1], ht_hi[:, h, 2 * i + b, 0:D],
                                               ALU.mult, ALU.subtract).then_inc(ht_lo_done, 1)

            with nc.vector.Fori(0, NB // 2 - 2) as i:
                ht_low(i)
            dve.wait_ge(u_in[0], 16)
            for pair in range(2):
                for j in (2 * pair, 2 * pair + 1):
                    numerators(0, 0, j, j)
                for j in (2 * pair, 2 * pair + 1):
                    low_part(j, j)
                ht_low(NB // 2 - 2 + pair)

            def head_inverse(group, b):
                dve.wait_ge(p_used, (group + 1) * NB)
                v.tensor_scalar(inv_l[:, b, :], ps[:, 4 * b:4 * b + QB, D], float(HEADS), None, ALU.mult
                                ).then_inc(sum4, 1)
                dve.wait_ge(sum4, group + 1)
                v.reciprocal(inv_l[:, b, :], inv_l[:, b, :]).then_inc(inv_done, 1)

            def quarter(q, first):
                for h in range(HEADS):
                    group = q * HEADS + h
                    if first:
                        dve.wait_ge(u_in[h], 16)
                    early = EARLY if first and h == 0 else 0
                    for j in range(early, NB):
                        step = group * NB + j
                        if j == 4 and not (first and h == 0):
                            head_inverse(group - 1, (h + 1) % 2)
                        numerators(q, h, j, step)
                        if not (first and h == 0 and j == early):
                            low_part((j - 1) % NB, step - 1)

            quarter(0, True)
            with nc.vector.Fori(1, NQ) as q:
                quarter(q, False)
            low_part(NB - 1, NQ * HEADS * NB - 1)
            head_inverse(NQ * HEADS - 1, 1)

            with nc.vector.Fori(0, NB // 4) as i:
                for k in range(4):
                    dve.wait_ge(o_ps, 4 * i + k + 1)
                    v.scalar_tensor_tensor(x[:, 4 * i + k, :], ps[:, k, 0:D], 0.0, x[:, 4 * i + k, :],
                                           ALU.max, ALU.add).then_inc(o_done, 1)


_INS = ["x", "adj", "L0_gnn_weight", "L0_gnn_bias", "L2_gnn_W", "L2_gnn_a", "L3_gnn_weight"]
_OUT = ((2048, 256), "float32")


def kernel(**inputs):
    import numpy as _np
    import concourse.bacc as _bacc
    from concourse import mybir as _mybir
    from concourse.bass_utils import run_bass_kernel_spmd as _run

    nc = _bacc.Bacc("TRN2", target_bir_lowering=False, num_devices=1)
    arrays, args = {}, []
    for name in _INS:
        a = _np.ascontiguousarray(inputs[name])
        arrays[f"in_{name}_dram"] = a
        args.append(nc.dram_tensor(f"in_{name}_dram", a.shape, _mybir.dt.from_np(a.dtype),
                                   kind="ExternalInput").ap())
    args.append(nc.dram_tensor("out_dram", _OUT[0], _mybir.dt.from_np(_np.dtype(_OUT[1])),
                               kind="ExternalOutput").ap())
    gnn_stack(nc, *args)
    r = _run(nc, [arrays], core_ids=[0])
    return r.results[0]["out_dram"]
```
